# Optimizing a Trainium2 kernel written in Bass

```python
import numpy as np
import jax
import jax.numpy as jnp

def _softmax(x, axis=-1):
    return jax.nn.softmax(x, axis=axis)

def _gelu(x):
    return jax.nn.gelu(x, approximate=True)

def _silu(x):
    return jax.nn.silu(x)

def _sigmoid(x):
    return jax.nn.sigmoid(x)

def _layernorm(x, axis=-1, eps=1e-05):
    m = jnp.mean(x, axis=axis, keepdims=True)
    v = jnp.var(x, axis=axis, keepdims=True)
    return (x - m) / jnp.sqrt(v + eps)

def _scatter_add(tgt, idx, src, axis=0):
    return tgt.at[idx].add(src)

def _segment_sum(src, seg, n):
    return jax.ops.segment_sum(src, seg, n)
kernel_name = 'mk_macaron_d1_jaxref_r8_8f35a6'

def setup_inputs(seed: int=0):
    np.random.seed(seed)
    _w = jnp.asarray

    def _L0_attn_setup():
        import jax, jax.numpy as jnp
        import numpy as np
        HIDDEN = 256
        NUM_HEADS = 16
        HEAD_DIM = HIDDEN // NUM_HEADS
        HARMONICS = 64

        def _holo_params(key, in_features, out_features, harmonics):
            kb, kp = jax.random.split(key)
            basis = jax.random.normal(kb, (harmonics, in_features), dtype=jnp.float32)
            basis = basis / jnp.linalg.norm(basis, axis=1, keepdims=True)
            phase = jax.random.normal(kp, (out_features, harmonics), dtype=jnp.float32) * 0.1
            amp = jnp.ones((out_features, harmonics), dtype=jnp.float32) / np.sqrt(harmonics).astype(np.float32)
            return (basis, phase, amp)

        def _holo_linear(x, basis, phase, amp):
            resonance = jnp.einsum('bsd,hd->bsh', x, basis)
            w = amp * jnp.cos(phase)
            return jnp.einsum('bsh,oh->bso', resonance, w)
        key = jax.random.key(seed)
        ks = jax.random.split(key, 5)
        hidden_states = jax.random.normal(ks[0], (2, 256, HIDDEN), dtype=jnp.float32)
        inp = {'hidden_states': hidden_states}
        for name, k in zip(('q', 'k', 'v', 'o'), ks[1:]):
            basis, phase, amp = _holo_params(k, HIDDEN, HIDDEN, HARMONICS)
            inp[f'basis_{name}'] = basis
            inp[f'phase_{name}'] = phase
            inp[f'amp_{name}'] = amp
        return inp
    _L0_attn_in = _L0_attn_setup()

    def _L0_ffn_setup():
        import jax, jax.numpy as jnp
        import numpy as np
        TOP_K = 2

        def moe_forward(x, w_gate_router, w_gate_proj, w_up_proj, w_down_proj):
            E = w_gate_router.shape[0]
            scores = jnp.einsum('bsd,ed->bse', x, w_gate_router)
            topk_scores, topk_idx = jax.lax.top_k(scores, TOP_K)
            topk_probs = jax.nn.softmax(topk_scores, axis=-1)
            weights = jnp.sum(topk_probs[..., None] * jax.nn.one_hot(topk_idx, E, dtype=x.dtype), axis=-2)
            gate = jnp.einsum('bsd,efd->bsef', x, w_gate_proj)
            up = jnp.einsum('bsd,efd->bsef', x, w_up_proj)
            hidden = jax.nn.silu(gate) * up
            out = jnp.einsum('bsef,edf,bse->bsd', hidden, w_down_proj, weights)
            return out
        key = jax.random.key(seed)
        k1, k2, k3, k4, k5 = jax.random.split(key, 5)
        B, S, D, E, F = (2, 128, 256, 8, 96)
        scale_in = 1.0 / np.sqrt(D)
        scale_ff = 1.0 / np.sqrt(F)
        return {'x': jax.random.normal(k1, (B, S, D), dtype=jnp.float32), 'w_gate_router': jax.random.normal(k2, (E, D), dtype=jnp.float32) * scale_in, 'w_gate_proj': jax.random.normal(k3, (E, F, D), dtype=jnp.float32) * scale_in, 'w_up_proj': jax.random.normal(k4, (E, F, D), dtype=jnp.float32) * scale_in, 'w_down_proj': jax.random.normal(k5, (E, D, F), dtype=jnp.float32) * scale_ff}
    _L0_ffn_in = _L0_ffn_setup()
    _d = {'L0_attn_hidden_states': _L0_attn_in['hidden_states'], 'L0_attn_basis_q': _L0_attn_in['basis_q'], 'L0_attn_phase_q': _L0_attn_in['phase_q'], 'L0_attn_amp_q': _L0_attn_in['amp_q'], 'L0_attn_basis_k': _L0_attn_in['basis_k'], 'L0_attn_phase_k': _L0_attn_in['phase_k'], 'L0_attn_amp_k': _L0_attn_in['amp_k'], 'L0_attn_basis_v': _L0_attn_in['basis_v'], 'L0_attn_phase_v': _L0_attn_in['phase_v'], 'L0_attn_amp_v': _L0_attn_in['amp_v'], 'L0_attn_basis_o': _L0_attn_in['basis_o'], 'L0_attn_phase_o': _L0_attn_in['phase_o'], 'L0_attn_amp_o': _L0_attn_in['amp_o'], 'L0_ffn_w_gate_router': _L0_ffn_in['w_gate_router'], 'L0_ffn_w_gate_proj': _L0_ffn_in['w_gate_proj'], 'L0_ffn_w_up_proj': _L0_ffn_in['w_up_proj'], 'L0_ffn_w_down_proj': _L0_ffn_in['w_down_proj']}
    _x0 = _d['L0_attn_hidden_states']
    _d['L0_attn_hidden_states'] = jax.random.normal(jax.random.fold_in(jax.random.key(seed), 1), (1, 1024, 256), dtype=_x0.dtype)
    del _x0
    return _d

def reference(L0_attn_hidden_states, L0_attn_basis_q, L0_attn_phase_q, L0_attn_amp_q, L0_attn_basis_k, L0_attn_phase_k, L0_attn_amp_k, L0_attn_basis_v, L0_attn_phase_v, L0_attn_amp_v, L0_attn_basis_o, L0_attn_phase_o, L0_attn_amp_o, L0_ffn_w_gate_router, L0_ffn_w_gate_proj, L0_ffn_w_up_proj, L0_ffn_w_down_proj):

    def _L0_attn_ref(hidden_states, basis_q, phase_q, amp_q, basis_k, phase_k, amp_k, basis_v, phase_v, amp_v, basis_o, phase_o, amp_o):
        import jax, jax.numpy as jnp
        import numpy as np
        HIDDEN = 256
        NUM_HEADS = 16
        HEAD_DIM = HIDDEN // NUM_HEADS
        HARMONICS = 64

        def _holo_params(key, in_features, out_features, harmonics):
            kb, kp = jax.random.split(key)
            basis = jax.random.normal(kb, (harmonics, in_features), dtype=jnp.float32)
            basis = basis / jnp.linalg.norm(basis, axis=1, keepdims=True)
            phase = jax.random.normal(kp, (out_features, harmonics), dtype=jnp.float32) * 0.1
            amp = jnp.ones((out_features, harmonics), dtype=jnp.float32) / np.sqrt(harmonics).astype(np.float32)
            return (basis, phase, amp)

        def _holo_linear(x, basis, phase, amp):
            resonance = jnp.einsum('bsd,hd->bsh', x, basis)
            w = amp * jnp.cos(phase)
            return jnp.einsum('bsh,oh->bso', resonance, w)
        bsz, seq_len, _ = hidden_states.shape
        q = _holo_linear(hidden_states, basis_q, phase_q, amp_q)
        k = _holo_linear(hidden_states, basis_k, phase_k, amp_k)
        v = _holo_linear(hidden_states, basis_v, phase_v, amp_v)
        q = q.reshape(bsz, seq_len, NUM_HEADS, HEAD_DIM).transpose(0, 2, 1, 3)
        k = k.reshape(bsz, seq_len, NUM_HEADS, HEAD_DIM).transpose(0, 2, 1, 3)
        v = v.reshape(bsz, seq_len, NUM_HEADS, HEAD_DIM).transpose(0, 2, 1, 3)
        scale = 1.0 / np.sqrt(HEAD_DIM).astype(np.float32)
        scores = jnp.einsum('bhqd,bhkd->bhqk', q, k) * scale
        attn = jax.nn.softmax(scores, axis=-1)
        out = jnp.einsum('bhqk,bhkd->bhqd', attn, v)
        out = out.transpose(0, 2, 1, 3).reshape(bsz, seq_len, HIDDEN)
        return _holo_linear(out, basis_o, phase_o, amp_o)

    def _L0_ffn_ref(x, w_gate_router, w_gate_proj, w_up_proj, w_down_proj):
        import jax, jax.numpy as jnp
        import numpy as np
        TOP_K = 2

        def moe_forward(x, w_gate_router, w_gate_proj, w_up_proj, w_down_proj):
            E = w_gate_router.shape[0]
            scores = jnp.einsum('bsd,ed->bse', x, w_gate_router)
            topk_scores, topk_idx = jax.lax.top_k(scores, TOP_K)
            topk_probs = jax.nn.softmax(topk_scores, axis=-1)
            weights = jnp.sum(topk_probs[..., None] * jax.nn.one_hot(topk_idx, E, dtype=x.dtype), axis=-2)
            gate = jnp.einsum('bsd,efd->bsef', x, w_gate_proj)
            up = jnp.einsum('bsd,efd->bsef', x, w_up_proj)
            hidden = jax.nn.silu(gate) * up
            out = jnp.einsum('bsef,edf,bse->bsd', hidden, w_down_proj, weights)
            return out
        return moe_forward(x, w_gate_router, w_gate_proj, w_up_proj, w_down_proj)
    x = L0_attn_hidden_states
    x = x + 0.5 * _L0_ffn_ref(_layernorm(x, axis=-1), L0_ffn_w_gate_router, L0_ffn_w_gate_proj, L0_ffn_w_up_proj, L0_ffn_w_down_proj)
    x = x + _L0_attn_ref(_layernorm(x, axis=-1), L0_attn_basis_q, L0_attn_phase_q, L0_attn_amp_q, L0_attn_basis_k, L0_attn_phase_k, L0_attn_amp_k, L0_attn_basis_v, L0_attn_phase_v, L0_attn_amp_v, L0_attn_basis_o, L0_attn_phase_o, L0_attn_amp_o)
    x = x + 0.5 * _L0_ffn_ref(_layernorm(x, axis=-1), L0_ffn_w_gate_router, L0_ffn_w_gate_proj, L0_ffn_w_up_proj, L0_ffn_w_down_proj)
    return x

_drawn_inputs = setup_inputs


def setup_inputs(seed=0):
    import zlib

    import numpy as np

    out = dict(_drawn_inputs(seed))
    spreads = {'L0_attn_amp_q': (0.125, 0.6),
     'L0_attn_amp_k': (0.125, 0.2),
     'L0_attn_amp_v': (0.125, 0.6),
     'L0_attn_amp_o': (0.125, 0.2)}
    factors = {'L0_attn_phase_q': 8.0,
     'L0_attn_phase_k': 8.0,
     'L0_attn_phase_v': 8.0,
     'L0_attn_phase_o': 8.0}
    for name, (base, spread) in spreads.items():
        noise = np.random.default_rng([zlib.crc32(name.encode()), seed]).standard_normal(out[name].shape)
        drawn = base * np.exp(spread * noise) if base else spread * noise
        out[name] = jnp.asarray(drawn.astype(out[name].dtype))
    for name, factor in factors.items():
        out[name] = (out[name] * factor).astype(out[name].dtype)
    return out
```

```python
from contextlib import ExitStack

import numpy as np

import concourse.bass as bass
from concourse import mybir

F32 = mybir.dt.float32
F32R = mybir.dt.float32r
U32 = mybir.dt.uint32
ALU = mybir.AluOpType
ACT = mybir.ActivationFunctionType
AX_X = mybir.AxisListType.X

P = 128
EPS = 1e-5
LN_FFN1, LN_ATT, LN_FFN2 = 0, 1, 2
Q, K, V, O = range(4)
TWO_PI = (6.28125, 0.0019350051879882812, 3.019916050448e-07)
ROUND = 12582912.0


def macaron_block(nc, x_in, basis, phase, amp, w_router, w_gate, w_up, w_down, out):
    _, S, D = x_in.shape
    E, F, _ = w_gate.shape
    HARM = basis[Q].shape[0]
    TILES = S // P
    BLOCKS = 2
    BT = TILES // BLOCKS
    BW = S // BLOCKS
    DH = D // P
    CH = E * F // P
    SUB = P // E
    HD = 16
    HEADS = D // HD
    GH = 4
    GROUPS = HEADS // GH
    UNITS = GROUPS * BLOCKS
    KT = TILES
    STEPS = UNITS * KT
    ITEMS = GH * BT
    PER_STEP = ITEMS // KT
    LEAD = 10 * PER_STEP
    SCALE = 1.0 / HD ** 0.5
    assert (S, D, HARM, BW, SUB) == (1024, 256, 64, 512, 16) and E * F == CH * P

    stages = []

    def ffn_stages(f):
        g0, g1 = 2 * f, 2 * f + 1
        l0, l1 = BLOCKS * 2 * f, BLOCKS * 2 * f + 1
        w = (f == 0)
        s = [("LN", l0)]
        s += [("LN", l1)] if not w else []
        s += [("XT", l0)]
        s += [("W_ROUTER",), ("W_GATE", 0), ("W_UP", 0)] if w else []
        s += [("ROUTE", g0), ("GU", g0, 0), ("TOP", g0)]
        s += [("W_GATE", 1), ("W_UP", 1), ("LN", l1)] if w else []
        s += [("GU", g0, 1), ("SPREAD", g0), ("GU", g0, 2)]
        s += [("W_GATE", 2), ("W_UP", 2)] if w else []
        s += [("GU", g0, 3), ("XT", l1), ("GU", g0, 4), ("ROUTE", g1), ("GU", g0, 5), ("TOP", g1)]
        s += [("W_DOWN", 0), ("W_DOWN", 1), ("W_DOWN", 2)] if w else []
        s += [("GU", g1, 0), ("SPREAD", g1), ("GU", g1, 1), ("DOWN", g0, 0), ("GU", g1, 2), ("DOWN", g0, 1)]
        s += [("ANGLE",)] if w else []
        s += [("GU", g1, 3), ("GU", g1, 4)]
        s += [("W_BASIS", 0), ("W_BASIS", 1), ("HOLO",)] if w else []
        s += [("GU", g1, 5)]
        s += [("W_HOLO", 0), ("W_HOLO", 1), ("LN", 2)] if w else []
        s += [("FLUSH", g1), ("DOWN", g1, 0), ("DOWN", g1, 1)]
        return s

    stages += ffn_stages(0)
    stages += [("XT", 2), ("LN", 3), ("RES", K, 0), ("RES", Q, 0), ("XT", 3), ("RES", K, 1), ("RES", Q, 1)]
    stages += [("QK", p, hf, b) for hf in range(2) for p in (K, Q) for b in range(2)]
    stages += [("RES", V, 0), ("RES", V, 1)] + [("V", i) for i in range(TILES // 2)]
    stages += [("ATTENTION",)]
    for b in range(BLOCKS):
        stages += [("AT", b), ("RES", O, b), ("Y", 2 * b), ("Y", 2 * b + 1)]
    stages += ffn_stages(1)

    t_no = {}
    for st in stages:
        for part in range(2 if st[0] in ("XT", "AT") else 0 if st[0] in ("LN", "GU", "DOWN", "ANGLE", "HOLO", "FLUSH", "ATTENTION") else 1):
            t_no[st + (part,)] = len(t_no)
    t_before_attention = t_no[("V", TILES // 2 - 1, 0)] + 1

    ring = [("maxima", 0)]
    m_step = {KT * u - 2: u for u in range(1, UNITS)}
    o_step = {KT * u + 1: u - 1 for u in range(1, UNITS)}
    for s in range(STEPS):
        ring += [("scores", s, j) for j in range(GH)]
        ring += [("maxima", m_step[s])] if s in m_step else []
        ring += [("turn", o_step[s])] if s in o_step else []
    ring += [("turn", UNITS - 1)]
    r_no = {use: n for n, use in enumerate(ring)}

    with ExitStack() as ctx:
        def sb(name, shape, dt=F32):
            return ctx.enter_context(nc.sbuf_tensor(name, shape, dt))

        def sem(name):
            return ctx.enter_context(nc.semaphore(name))

        x = sb("x", [P, TILES, D])
        xn = sb("xn", [P, TILES, D])
        xt_hi = sb("xt_hi", [P, DH, S], F32R)
        xt_lo = sb("xt_lo", [P, DH, S], F32R)
        gate_hi = sb("gate_hi", [P, CH, DH, P], F32R)
        gate_lo = sb("gate_lo", [P, CH, DH, P], F32R)
        up_hi = sb("up_hi", [P, CH, DH, P], F32R)
        up_lo = sb("up_lo", [P, CH, DH, P], F32R)
        down_hi = sb("down_hi", [P, CH, D], F32R)
        down_lo = sb("down_lo", [P, CH, D], F32R)
        router_hi = sb("router_hi", [P, DH, E], F32R)
        router_lo = sb("router_lo", [P, DH, E], F32R)
        basis_hi = sb("basis_hi", [P, 4, DH, P], F32R)
        basis_lo = sb("basis_lo", [P, 4, DH, P], F32R)
        holo_hi = sb("holo_hi", [P, 4, 2, P], F32R)
        holo_lo = sb("holo_lo", [P, 4, 2, P], F32R)
        res = sb("res", [P, 3, S], F32R)
        v_mem = sb("v_mem", [P, KT * HEADS * 32])
        v1 = v_mem[:, :].rearrange("p (k h c) -> p k h c", k=KT, h=HEADS)
        small = 4 * 2 * HARM
        basis_in = v_mem[:, 0:4 * D].rearrange("p (w d) -> p w d", w=4)
        phase_in = v_mem[:, 4 * D:4 * D + small]
        amp_in = v_mem[:, 4 * D + small:4 * D + 2 * small]
        cos_t = v_mem[:, 4 * D + 2 * small:4 * D + 3 * small]
        cos_n = v_mem[:, 4 * D + 3 * small:4 * D + 4 * small]
        QUARTER = GH * S
        MAX_ROW = 96
        big = sb("big", [P, 4 * QUARTER], F32R)
        hid = big[:, 0:4 * CH * BW].rearrange("p (g a m t) -> p g a m t", g=2, a=2, m=CH)
        ks = [big[0:MAX_ROW + 2, i * QUARTER:(i + 1) * QUARTER].rearrange("p (j t) -> p j t", j=GH) for i in (0, 2)]
        qs = [big[0:MAX_ROW + 2, i * QUARTER:(i + 1) * QUARTER].rearrange("p (b j t) -> p b j t", b=BLOCKS, j=GH) for i in (1, 3)]
        qk_parts = big[:, 2 * QUARTER:4 * QUARTER].rearrange("p (w a h t) -> p w a h t", w=2, a=2, h=2)
        many = sb("many", [P, 3 * CH * D])
        gate_in = many[:, 0:CH * D].rearrange("p (m d) -> p m d", m=CH)
        up_in = many[:, CH * D:2 * CH * D].rearrange("p (m d) -> p m d", m=CH)
        down_in = many[:, 2 * CH * D:3 * CH * D].rearrange("p (h e f) -> p h e f", h=DH, e=E)
        holo_in = many[:, 0:1024].rearrange("p (w h c r) -> p w h c r", w=4, h=2, c=2)
        probs = many[:, 0:8 * BW].rearrange("p (n t) -> p n t", n=8)
        router_in = sb("router_in", [E, D])
        ident = sb("ident", [P, P])
        zeros = sb("zeros", [P, P])
        expert_no = sb("expert_no", [P, BT, E])
        minus_half = sb("minus_half", [P, BT])
        stats = sb("stats", [P, BT, 6])
        mean_var = sb("mean_var", [P, BT, 2])
        var_eps = sb("var_eps", [P, BT])
        rstd = sb("rstd", [P, BT])
        NH = 5
        feat = sb("feat", [P, NH, BW])
        route_w = sb("route_w", [P, 2, BW])
        score_t = sb("score_t", [E, BW])
        score = sb("score", [P, BT, E])
        top8 = sb("top8", [P, BT, E])
        top_no = sb("top_no", [P, BT, E], U32)
        top_nf = sb("top_nf", [P, BT, 2])
        gap = sb("gap", [P, BT, 1])
        second = sb("second", [P, BT, 1])
        prob = sb("prob", [P, 2, BT, 1])
        chosen = sb("chosen", [P, 2, BT, E])
        spread = sb("spread", [P, BT, E, SUB])
        neg_max = sb("neg_max", [P, 2, ITEMS])
        max_parts = sb("max_parts", [P, 2 * ITEMS], F32R)
        max_rows = sb("max_rows", [2 * ITEMS, P])
        pv_t = feat[:, 0, :]
        pv_q = feat[:, 1, :].rearrange("p (i j c) -> p i j c", i=BT, j=GH)
        rden = sb("rden", [P, BT, GH])
        bank = [ctx.enter_context(nc.psum_tensor(f"bank{i}", [P, 512], F32)) for i in range(4)]
        pair = [ctx.enter_context(nc.psum_tensor(f"pair{i}", [P, 2, 512], F32)) for i in range(2)]
        gate_b = [bank[0], bank[1]]
        up_b = [bank[2], bank[3]]
        down_b = [pair[0][:, 0, :], pair[0][:, 1, :]]
        t_b = [pair[1][:, 0, :], pair[1][:, 1, :]]
        ring_b = bank[0:3]
        pv_b = bank[3]
        qk_dram = nc.dram_tensor("qk_parts_dram", (2, 2, D, S), F32).ap()
        x_in_s = [sem(f"x_loaded{b}") for b in range(BLOCKS)]
        gate_in_s, up_in_s = sem("gate_loaded"), sem("up_loaded")
        down_in_s, router_in_s = sem("down_loaded"), sem("router_loaded")
        holo_in_s, basis_in_s = sem("phase_amp_loaded"), sem("basis_loaded")
        const_s = sem("constants_ready")
        t_full = sem("t_full")
        t_free = [sem("t_free0"), sem("t_free1")]
        hi_s = sem("hi_part_ready")
        step_s = sem("vector_step")
        var_s, rstd_s, xn_s = sem("var_ready"), sem("rstd_ready"), sem("xn_ready")
        gate_full, up_full = sem("gate_full"), sem("up_full")
        tanh_s, silu_s = sem("tanh_ready"), sem("silu_ready")
        gated_s, weighed_s = sem("gated_ready"), sem("weighed_ready")
        hid_hi_s, hid_lo_s = sem("hid_hi_ready"), sem("hid_lo_ready")
        down_full, x_s = sem("down_full"), sem("x_updated")
        gap_s, second_s, spread_s = sem("gap_ready"), sem("second_ready"), sem("spread_ready")
        angle_s, sine_s, holo_s = sem("angle_ready"), sem("sine_ready"), sem("holo_ready")
        qk_out_s = [sem("qk_stored0"), sem("qk_stored1")]
        ones_s, zero_rows_s = sem("ones_ready"), sem("zero_rows_ready")
        stack_s = [sem("stack_loaded0"), sem("stack_loaded1")]
        item_full, item_read = sem("item_full"), sem("item_read")
        max_parts_s, max_in_s = sem("max_parts_ready"), sem("max_rows_placed")
        ring_full, ring_read = sem("ring_full"), sem("ring_read")
        pv_s, pv_read = sem("pv_steps_done"), sem("pv_read")
        att_s = sem("attention_unit_ready")
        out_s = sem("out_stored")

        x_tok = x_in.rearrange("a (p i) d -> (a p) i d", p=P)
        out_tok = out.rearrange("a (p i) d -> (a p) i d", p=P)
        gate_rows = w_gate.rearrange("e f d -> (e f) d").rearrange("(p m) d -> p m d", m=CH)
        up_rows = w_up.rearrange("e f d -> (e f) d").rearrange("(p m) d -> p m d", m=CH)

        def freed(eng, n):
            eng.wait_ge(t_free[n % 2], n // 2 + 1)

        def block_of(b):
            return slice(b * BW, (b + 1) * BW)

        def tiles_of(b):
            return slice(b * BT, (b + 1) * BT)

        def split_of(st, part):
            kind, w = st[0], st[1] if len(st) > 1 else 0
            if kind in ("XT", "AT"):
                return xt_hi[:, part, block_of(w % BLOCKS)], xt_lo[:, part, block_of(w % BLOCKS)]
            if kind == "W_ROUTER":
                return router_hi[:, :, :], router_lo[:, :, :]
            two = slice(2 * w, 2 * w + 2)
            if kind == "W_GATE":
                return gate_hi[:, two, :, :], gate_lo[:, two, :, :]
            if kind == "W_UP":
                return up_hi[:, two, :, :], up_lo[:, two, :, :]
            if kind == "W_DOWN":
                return down_hi[:, two, :], down_lo[:, two, :]
            if kind == "W_BASIS":
                return basis_hi[:, two, :, :], basis_lo[:, two, :, :]
            if kind == "W_HOLO":
                return holo_hi[:, two, :, :], holo_lo[:, two, :, :]
            if kind == "QK":
                _, w, hf, b = st
                return qk_parts[:, w, 0, hf, block_of(b)], qk_parts[:, w, 1, hf, block_of(b)]

        def seen_as(bank_ap, like):
            dims = list(like.shape)[1:]
            flat = bank_ap[:, 0:int(np.prod(dims))]
            if len(dims) == 1:
                return flat
            if len(dims) == 2:
                return flat.rearrange("p (a b) -> p a b", a=dims[0])
            return flat.rearrange("p (a b c) -> p a b c", a=dims[0], b=dims[1])

        block = ctx.enter_context(nc.Block())

        @block.sync
        def _(sp):
            sp.dma_start(x[:, 0:BT, :], x_tok[:, 0:BT, :]).then_inc(x_in_s[0], 16)
            sp.dma_start(gate_in, gate_rows).then_inc(gate_in_s, 16)
            sp.dma_start(router_in[:, :], w_router).then_inc(router_in_s, 16)
            sp.dma_start(up_in, up_rows).then_inc(up_in_s, 16)
            sp.dma_start(x[:, BT:TILES, :], x_tok[:, BT:TILES, :]).then_inc(x_in_s[1], 16)
            for h in range(DH):
                sp.dma_start(down_in[:, h, :, :],
                             w_down.rearrange("e (h p) f -> h p e f", h=DH)[h]).then_inc(down_in_s, 16)
            for w in range(4):
                sp.dma_start(phase_in[:, w * 2 * HARM:(w + 1) * 2 * HARM].rearrange("p (h r) -> p h r", h=2), phase[w].rearrange("(h p) r -> p h r", h=2)).then_inc(holo_in_s, 16)
                sp.dma_start(amp_in[:, w * 2 * HARM:(w + 1) * 2 * HARM].rearrange("p (h r) -> p h r", h=2), amp[w].rearrange("(h p) r -> p h r", h=2)).then_inc(holo_in_s, 16)
            for w in range(4):
                for c in range(2):
                    sp.dma_start(basis_in[c * HARM:(c + 1) * HARM, w, :], basis[w]).then_inc(basis_in_s, 16)
            for hf in range(2):
                for w in (K, Q):
                    for b in range(BLOCKS):
                        freed(sp, t_no[("QK", w, hf, b, 0)])
                    sp.dma_start(qk_dram[w][:, hf * P:(hf + 1) * P, :].rearrange("a p t -> p a t"),
                                 qk_parts[:, w, :, hf, :].bitcast(F32)).then_inc(qk_out_s[hf], 16)

            def load_stacks(hg):
                sp.wait_ge(qk_out_s[0], 32)
                if hg == 1:
                    sp.wait_ge(qk_out_s[1], 32)
                if hg >= 2:
                    sp.wait_ge(pv_s, 2 * KT * (hg - 1))
                rows = slice(hg * GH * HD, (hg + 1) * GH * HD)
                for c, part in enumerate((0, 0, 1, 1)):
                    sp.dma_start(ks[hg % 2][c * HD:(c + 1) * HD, :, :].bitcast(F32),
                                 qk_dram[K][part, rows, :].rearrange("(j d) t -> d j t", j=GH)
                                 ).then_inc(stack_s[hg % 2], 16)
                for b in range(BLOCKS):
                    for c, part in enumerate((0, 1, 0, 1)):
                        sp.dma_start(qs[hg % 2][c * HD:(c + 1) * HD, b, :, :].bitcast(F32),
                                     qk_dram[Q][part, rows, block_of(b)].rearrange("(j d) t -> d j t", j=GH)
                                     ).then_inc(stack_s[hg % 2], 16)

            load_stacks(0)
            load_stacks(1)
            for u in range(UNITS):
                hg, b = u // BLOCKS, u % BLOCKS
                sp.wait_ge(ring_read, r_no[("maxima", u)] + 1)
                for part in range(2):
                    sp.dma_start(qs[hg % 2][MAX_ROW + part:MAX_ROW + part + 1, b, :, :].bitcast(F32)
                                 .rearrange("o j (i c) -> o (j i) c", c=P),
                                 max_rows[part * ITEMS:(part + 1) * ITEMS, :]).then_inc(max_in_s, 16)
                if u in (2, 4):
                    load_stacks(u // 2 + 1)
            for b in range(BLOCKS):
                sp.wait_ge(x_s, 2 * BLOCKS + 2 * (b + 1))
                sp.dma_start(out_tok[:, tiles_of(b), :], x[:, tiles_of(b), :]).then_inc(out_s, 16)
            sp.wait_ge(out_s, 16 * BLOCKS)

        @block.gpsimd
        def _(pool):
            pool.memset(zeros[:, :], 0.0).then_inc(const_s, 1)
            pool.wait_ge(const_s, 1)
            pool.affine_select(out=ident[:, :], in_=zeros[:, :], compare_op=ALU.not_equal, fill=1.0, base=0,
                               pattern=[[-1, P]], channel_multiplier=1).then_inc(const_s, 1)
            pool.memset(minus_half[:, :], -0.5).then_inc(const_s, 1)
            for e in range(E):
                pool.memset(expert_no[:, :, e:e + 1], float(e)).then_inc(const_s, 1)

            def hid_lo(n):
                g, m = n // CH, n % CH
                pool.wait_ge(hid_hi_s, n + 1)
                pool.tensor_tensor(hid[:, g % 2, 1, m, :], feat[:, n % NH, :],
                                   hid[:, g % 2, 0, m, :].bitcast(F32), ALU.subtract).then_inc(hid_lo_s, 1)

            def weigh(n):
                g, m = n // CH, n % CH
                pool.wait_ge(gated_s, n + 1)
                if m == 0:
                    freed(pool, t_no[("SPREAD", g, 0)])
                pool.tensor_tensor(feat[:, n % NH, :], feat[:, n % NH, :], route_w[:, g % 2, :],
                                   ALU.mult).then_inc(weighed_s, 1)

            for st in stages:
                if st[0] == "LN":
                    l = st[1]
                    pool.wait_ge(var_s, l + 1)
                    if l == 0:
                        pool.wait_ge(const_s, 3)
                    else:
                        pool.wait_ge(xn_s, l)
                    pool.tensor_tensor(rstd[:, :], var_eps[:, :], minus_half[:, :], ALU.pow).then_inc(rstd_s, 1)
                elif st[0] == "GU":
                    n = st[1] * CH + st[2]
                    first = n // (2 * CH) * 2 * CH
                    if n > first:
                        weigh(n - 1)
                    if n > first + 1:
                        hid_lo(n - 2)
                elif st[0] == "FLUSH":
                    n = (st[1] + 1) * CH
                    weigh(n - 1)
                    hid_lo(n - 2)
                    hid_lo(n - 1)
                elif st[0] == "ATTENTION":
                    freed(pool, t_no[("W_HOLO", 1, 0)])
                    pool.memset(v1[:, :, :, HD:32], 1.0).then_inc(ones_s, 1)
                    pool.wait_ge(ones_s, 1)
                    pool.wait_ge(x_s, 4)
                    for hg in range(GROUPS):
                        if hg == 1:
                            pool.wait_ge(qk_out_s[0], 32)
                            pool.wait_ge(qk_out_s[1], 32)
                        if hg < 2:
                            pool.memset(ks[hg][MAX_ROW:MAX_ROW + 2, :, :].bitcast(F32), 1.0).then_inc(ones_s, 1)
                            pool.wait_ge(ones_s, 3 * hg + 2)
                            pool.memset(ks[hg][64:MAX_ROW, :, :].bitcast(F32), 0.0).then_inc(ones_s, 1)
                            pool.wait_ge(ones_s, 3 * hg + 3)
                            pool.memset(qs[hg][64:MAX_ROW, :, :, :].bitcast(F32), 0.0).then_inc(ones_s, 1)
                            pool.wait_ge(ones_s, 3 * hg + 4)
                        else:
                            pool.wait_ge(pv_s, 2 * KT * (hg - 1))
                        pool.memset(qs[hg % 2][MAX_ROW:MAX_ROW + 2, :, :, :].bitcast(F32), 0.0).then_inc(zero_rows_s, 1)
                        pool.wait_ge(zero_rows_s, hg + 1)

        @block.scalar
        def _(act):
            def hid_hi(n):
                g, m = n // CH, n % CH
                act.wait_ge(weighed_s, n + 1)
                act.copy(hid[:, g % 2, 0, m, :], feat[:, n % NH, :]).then_inc(hid_hi_s, 1)

            def pv_out(u):
                act.wait_ge(pv_s, KT * (u + 1))
                act.copy(pv_t, pv_b[:, :]).then_inc(pv_read, 1)

            def attention():
                for use in ring:
                    n = r_no[use]
                    src = ring_b[n % 3]
                    if use[0] == "turn" and use[1] == UNITS - 1:
                        pv_out(UNITS - 1)
                    act.wait_ge(ring_full, n + 1)
                    if use[0] == "maxima":
                        if use[1] >= 1:
                            act.wait_ge(max_in_s, 32 * use[1])
                        act.copy(max_rows[:, :], src[0:2 * ITEMS, 0:P]).then_inc(ring_read, 1)
                    elif use[0] == "turn":
                        if use[1] >= 1:
                            act.wait_ge(att_s, use[1])
                        act.copy(pv_q, src[:, :].rearrange("p (i j c) -> p i j c", i=BT, j=GH)
                                 ).then_inc(ring_read, 1)
                    else:
                        _, s, j = use
                        if s >= 2:
                            act.wait_ge(pv_s, s - 1)
                        act.activation(probs[:, (GH * s + j) % 8, :], src[:, :], ACT.Exp,
                                       scale=SCALE).then_inc(ring_read, 1)
                        if j == 2 and s % KT == 0 and s > 0:
                            pv_out(s // KT - 1)

            for st in stages:
                kind = st[0]
                if kind in ("XT", "AT", "W_ROUTER", "W_GATE", "W_UP", "W_DOWN", "W_BASIS", "W_HOLO", "QK"):
                    for part in range(2 if kind in ("XT", "AT") else 1):
                        n = t_no[st + (part,)]
                        hi, _ = split_of(st, part)
                        act.wait_ge(t_full, n + 1)
                        act.copy(hi, seen_as(t_b[n % 2], hi)).then_inc(hi_s, 1)
                elif kind == "RES":
                    _, w, b = st
                    n = t_no[st + (0,)]
                    act.wait_ge(t_full, n + 1)
                    act.copy(res[:, w % 3, block_of(b)], t_b[n % 2]).then_inc(hi_s, 1)
                elif kind == "ROUTE":
                    n = t_no[st + (0,)]
                    act.wait_ge(t_full, n + 1)
                    act.copy(score_t[:, :], t_b[n % 2][0:E, :]).then_inc(t_free[n % 2], 1)
                elif kind == "TOP":
                    act.wait_ge(gap_s, st[1] + 1)
                    act.activation(second[:, :, :], gap[:, :, :], ACT.Exp).then_inc(second_s, 1)
                elif kind == "SPREAD":
                    n = t_no[st + (0,)]
                    if st[1] >= 2:
                        act.wait_ge(weighed_s, CH * (st[1] - 1))
                    act.wait_ge(t_full, n + 1)
                    act.copy(route_w[:, st[1] % 2, :], t_b[n % 2]).then_inc(t_free[n % 2], 1)
                elif kind == "GU":
                    _, g, m = st
                    n = g * CH + m
                    act.wait_ge(gate_full, n + 1)
                    if n >= NH:
                        act.wait_ge(hid_lo_s, n - NH + 1)
                    act.activation(feat[:, n % NH, :], gate_b[n % 2][:, :], ACT.Tanh, scale=0.5).then_inc(tanh_s, 1)
                    if n > n // (2 * CH) * 2 * CH + 1:
                        hid_hi(n - 2)
                elif kind == "FLUSH":
                    hid_hi((st[1] + 1) * CH - 2)
                    hid_hi((st[1] + 1) * CH - 1)
                elif kind == "ANGLE":
                    act.wait_ge(angle_s, 1)
                    act.activation(cos_n, cos_t, ACT.Sin, scale=0.5).then_inc(sine_s, 1)
                elif kind == "V":
                    n = t_no[st + (0,)]
                    act.wait_ge(t_full, n + 1)
                    act.copy(v1[:, 2 * st[1]:2 * st[1] + 2, :, 0:HD],
                             t_b[n % 2].rearrange("p (i h c) -> p i h c", i=2, h=HEADS)).then_inc(t_free[n % 2], 1)
                elif kind == "ATTENTION":
                    attention()

        @block.vector
        def _(dve):
            steps = [0]

            def link(ins):
                steps[0] += 1
                ins.then_inc(step_s, 1)
                dve.wait_ge(step_s, steps[0])

            hi_no = [0]

            def lo_part(n, lo, hi, src):
                hi_no[0] += 1
                dve.wait_ge(hi_s, hi_no[0])
                dve.tensor_tensor(lo, src, hi.bitcast(F32), ALU.subtract).then_inc(t_free[n % 2], 1)

            def layer_norm(l):
                b = l % BLOCKS
                if l < 2:
                    dve.wait_ge(x_in_s[b], 16)
                elif l < 4:
                    dve.wait_ge(x_s, 2 * (b + 1))
                else:
                    freed(dve, t_no[("Y", 2 * b + 1, 0)])
                for i in range(BT):
                    link(dve.bn_stats(stats[:, i, :], x[:, b * BT + i, :]))
                for i in range(BT):
                    link(dve.bn_aggr(mean_var[:, i, :], stats[:, i, :]))
                dve.tensor_scalar(var_eps[:, :], mean_var[:, :, 1], EPS, None, ALU.add).then_inc(var_s, 1)
                dve.wait_ge(rstd_s, l + 1)
                for i in range(BT):
                    ins = dve.tensor_scalar(xn[:, b * BT + i, :], x[:, b * BT + i, :], mean_var[:, i, 0:1],
                                            rstd[:, i:i + 1], ALU.subtract, ALU.mult)
                ins.then_inc(xn_s, 1)

            def route(g, n):
                dve.wait_ge(t_full, n + 1)
                if g == 0:
                    dve.wait_ge(const_s, 3 + E)
                ins = dve.tensor_copy(score[:, :, :], t_b[n % 2][:, 0:BT * E].rearrange("p (i e) -> p i e", i=BT))
                ins.then_inc(t_free[n % 2], 1)
                freed(dve, n)
                for i in range(BT):
                    link(dve.max(top8[:, i, :], score[:, i, :]))
                for i in range(BT):
                    link(dve.max_index(top_no[:, i, :], top8[:, i, :], score[:, i, :]))
                dve.tensor_tensor(gap[:, :, :], top8[:, :, 1:2], top8[:, :, 0:1], ALU.subtract).then_inc(gap_s, 1)
                link(dve.tensor_copy(top_nf[:, :, :], top_no[:, :, 0:2]))
                for c in range(2):
                    link(dve.tensor_tensor(chosen[:, c, :, :], expert_no[:, :, :],
                                           top_nf[:, :, c:c + 1].broadcast_to([P, BT, E]), ALU.is_equal))
                dve.wait_ge(second_s, g + 1)
                link(dve.tensor_scalar(prob[:, 1, :, :], second[:, :, :], 4.0, 4.0, ALU.mult, ALU.add))
                link(dve.reciprocal(prob[:, 0, :, :], prob[:, 1, :, :]))
                link(dve.tensor_tensor(prob[:, 1, :, :], prob[:, 0, :, :], second[:, :, :], ALU.mult))
                for c in range(2):
                    link(dve.tensor_tensor(chosen[:, c, :, :], chosen[:, c, :, :],
                                           prob[:, c, :, :].broadcast_to([P, BT, E]), ALU.mult))
                link(dve.tensor_tensor(chosen[:, 0, :, :], chosen[:, 0, :, :], chosen[:, 1, :, :], ALU.add))
                dve.tensor_copy(spread[:, :, :, :].rearrange("p i e r -> p (i e) r"),
                                chosen[:, 0, :, :].rearrange("p i e -> p (i e)").unsqueeze(2)
                                .broadcast_to([P, BT * E, SUB])).then_inc(spread_s, 1)

            def normalise(u):
                hg, b = u // BLOCKS, u % BLOCKS
                dve.wait_ge(ring_read, r_no[("turn", u)] + 1)
                link(dve.reciprocal(rden[:, :, :], pv_q[:, :, :, HD]))
                dve.tensor_tensor(xn[:, tiles_of(b), hg * GH * HD:(hg + 1) * GH * HD]
                                  .rearrange("p i (j c) -> p i j c", j=GH),
                                  pv_q[:, :, :, 0:HD],
                                  rden[:, :, :].unsqueeze(3).broadcast_to([P, BT, GH, HD]), ALU.mult).then_inc(att_s, 1)

            def attention():
                at_item = {LEAD + PER_STEP * (KT * (u + 1) + 2): u for u in range(UNITS)}
                done = []
                for it in range(UNITS * ITEMS):
                    u, i = it // ITEMS, it % ITEMS
                    dve.wait_ge(item_full, it + 1)
                    dve.tensor_reduce(neg_max[:, u % 2, i:i + 1], pair[it % 2][:, :, :].rearrange("p a b -> p (a b)"),
                                      AX_X, ALU.max, negate=True).then_inc(item_read, 1)
                    if i == ITEMS - 1:
                        dve.wait_ge(item_read, it + 1)
                        if u >= 1:
                            dve.wait_ge(ring_full, r_no[("maxima", u - 1)] + 1)
                        link(dve.tensor_copy(max_parts[:, 0:ITEMS], neg_max[:, u % 2, :]))
                        dve.tensor_tensor(max_parts[:, ITEMS:2 * ITEMS], neg_max[:, u % 2, :],
                                          max_parts[:, 0:ITEMS].bitcast(F32), ALU.subtract).then_inc(max_parts_s, 1)
                    if it in at_item:
                        normalise(at_item[it])
                        done.append(at_item[it])
                for u in range(UNITS):
                    if u not in done:
                        normalise(u)

            for st in stages:
                kind = st[0]
                if kind == "LN":
                    layer_norm(st[1])
                elif kind in ("XT", "AT", "W_ROUTER", "W_GATE", "W_UP", "W_DOWN", "W_BASIS", "W_HOLO", "QK"):
                    for part in range(2 if kind in ("XT", "AT") else 1):
                        n = t_no[st + (part,)]
                        hi, lo = split_of(st, part)
                        lo_part(n, lo, hi, seen_as(t_b[n % 2], hi))
                elif kind == "RES":
                    _, w, b = st
                    n = t_no[st + (0,)]
                    both = res[HARM:2 * HARM, w % 3, block_of(b)]
                    lo_part(n, both, both, t_b[n % 2][HARM:2 * HARM, :])
                elif kind == "TOP":
                    route(st[1], t_no[st + (0,)])
                elif kind == "GU":
                    _, g, m = st
                    n = g * CH + m
                    dve.wait_ge(tanh_s, n + 1)
                    dve.scalar_tensor_tensor(out=feat[:, n % NH, :], in0=feat[:, n % NH, :], scalar=1.0,
                                             in1=gate_b[n % 2][:, :], op0=ALU.add, op1=ALU.mult).then_inc(silu_s, 1)
                    dve.wait_ge(silu_s, n + 1)
                    dve.wait_ge(up_full, n + 1)
                    dve.tensor_tensor(feat[:, n % NH, :], feat[:, n % NH, :], up_b[n % 2][:, :],
                                      ALU.mult).then_inc(gated_s, 1)
                elif kind == "DOWN":
                    _, g, i = st
                    dve.wait_ge(down_full, 2 * g + i + 1)
                    tiles = slice(g % 2 * BT + 2 * i, g % 2 * BT + 2 * i + 2)
                    dve.tensor_tensor(x[:, tiles, :], x[:, tiles, :],
                                      down_b[i].rearrange("p (a d) -> p a d", a=2), ALU.add).then_inc(x_s, 1)
                elif kind == "Y":
                    n = t_no[st + (0,)]
                    tiles = slice(2 * st[1], 2 * st[1] + 2)
                    dve.wait_ge(t_full, n + 1)
                    dve.tensor_tensor(x[:, tiles, :], x[:, tiles, :],
                                      t_b[n % 2].rearrange("p (a d) -> p a d", a=2), ALU.add).then_inc(t_free[n % 2], 1)
                elif kind == "ANGLE":
                    ph = phase_in
                    dve.wait_ge(holo_in_s, 16 * 8)
                    link(dve.tensor_scalar(cos_n, ph, 1.0 / (2.0 * np.pi), ROUND, ALU.mult, ALU.add))
                    link(dve.tensor_scalar(cos_n, cos_n, ROUND, None, ALU.subtract))
                    link(dve.scalar_tensor_tensor(out=cos_t, in0=cos_n, scalar=-TWO_PI[0], in1=ph,
                                                  op0=ALU.mult, op1=ALU.add))
                    link(dve.scalar_tensor_tensor(out=cos_t, in0=cos_n, scalar=-TWO_PI[1], in1=cos_t,
                                                  op0=ALU.mult, op1=ALU.add))
                    dve.scalar_tensor_tensor(out=cos_t, in0=cos_n, scalar=-TWO_PI[2], in1=cos_t,
                                             op0=ALU.mult, op1=ALU.add).then_inc(angle_s, 1)
                elif kind == "HOLO":
                    dve.wait_ge(sine_s, 1)
                    link(dve.tensor_tensor(cos_t, cos_n, cos_n, ALU.mult))
                    link(dve.tensor_scalar(cos_n, cos_t, -2.0, 1.0, ALU.mult, ALU.add))
                    for c in range(2):
                        dve.tensor_tensor(holo_in[:, :, :, c, :].rearrange("p w h r -> p (w h) r"),
                                          cos_n.rearrange("p (a r) -> p a r", r=HARM),
                                          amp_in.rearrange("p (a r) -> p a r", r=HARM), ALU.mult).then_inc(holo_s, 1)
                elif kind == "ATTENTION":
                    attention()

        @block.tensor
        def _(pe):
            THREE = ((0, 0), (0, 1), (1, 0))

            def take(n):
                if n >= 2:
                    freed(pe, n - 2)
                return t_b[n % 2]

            def product(dst, stationary, moving, last_of_group=True):
                for dh in range(DH):
                    for c, (a, b) in enumerate(THREE):
                        ins = pe.matmul(dst, stationary[a](dh), moving[b](dh),
                                        start=(dh == 0 and c == 0), stop=(dh == DH - 1 and c == 2))
                return ins

            def xt(b):
                return [lambda dh: xt_hi[:, dh, block_of(b)], lambda dh: xt_lo[:, dh, block_of(b)]]

            def turned(n, sources, width=P, rows=P):
                dst = take(n)
                for c, src in enumerate(sources):
                    ins = pe.transpose(dst[:, c * width:(c + 1) * width], src, ident[0:rows, 0:rows])
                ins.then_inc(t_full, 1)

            def item(it):
                u, i = it // ITEMS, it % ITEMS
                hg, b = u // BLOCKS, u % BLOCKS
                j, tile = i // BT, i % BT
                if it == 0:
                    pe.wait_ge(x_s, 4)
                if it == 1:
                    for n in (t_before_attention - 2, t_before_attention - 1):
                        freed(pe, n)
                if b == 0 and i == 0:
                    pe.wait_ge(stack_s[hg % 2], 12 * 16 * (hg // 2 + 1))
                    pe.wait_ge(zero_rows_s, hg + 1)
                if it >= 2:
                    pe.wait_ge(item_read, it - 1)
                for c in range(2):
                    ins = pe.matmul(pair[it % 2][:, c, :], qs[hg % 2][:, b, j, tile * P:(tile + 1) * P],
                                    ks[hg % 2][:, j, c * BW:(c + 1) * BW], start=True, stop=True)
                ins.then_inc(item_full, 1)

            def ring_take(use):
                n = r_no[use]
                if n >= 3:
                    pe.wait_ge(ring_read, n - 2)
                return ring_b[n % 3]

            def maxima(u):
                pe.wait_ge(max_parts_s, u + 1)
                dst = ring_take(("maxima", u))
                pe.transpose(dst[0:2 * ITEMS, 0:P], max_parts[:, :].bitcast(F32), ident[:, :]).then_inc(ring_full, 1)

            def scores(s, j):
                u, kt = s // KT, s % KT
                hg, b = u // BLOCKS, u % BLOCKS
                if kt == 0 and j == 0:
                    pe.wait_ge(max_in_s, 32 * (u + 1))
                dst = ring_take(("scores", s, j))
                pe.matmul(dst[:, :], ks[hg % 2][:, j, kt * P:(kt + 1) * P], qs[hg % 2][:, b, j, :],
                          start=True, stop=True).then_inc(ring_full, 1)

            def weigh_values(s):
                u, kt = s // KT, s % KT
                if s == 0:
                    for i in (TILES // 2 - 2, TILES // 2 - 1):
                        freed(pe, t_no[("V", i, 0)])
                    pe.wait_ge(ones_s, 1)
                if kt == 0 and u >= 1:
                    pe.wait_ge(pv_read, u)
                pe.wait_ge(ring_read, r_no[("scores", s, GH - 1)] + 1)
                for j in range(GH):
                    ins = pe.matmul(pv_b[32 * j:32 * j + 32, :], v1[:, kt, u // BLOCKS * GH + j, :],
                                    probs[:, (GH * s + j) % 8, :], start=(kt == 0), stop=(kt == KT - 1))
                ins.then_inc(pv_s, 1)

            def turn(u):
                pe.wait_ge(pv_read, u + 1)
                dst = ring_take(("turn", u))
                for i in range(BT):
                    ins = pe.transpose(dst[:, i * P:(i + 1) * P], pv_t[:, i * P:(i + 1) * P], ident[:, :])
                ins.then_inc(ring_full, 1)

            def attention():
                items = UNITS * ITEMS
                for it in range(LEAD):
                    item(it)
                    if it == ITEMS + 1:
                        maxima(0)
                for s in range(STEPS):
                    ahead = [it for it in range(LEAD + PER_STEP * s, LEAD + PER_STEP * (s + 1)) if it < items]
                    scores(s, 0)
                    scores(s, 1)
                    if ahead:
                        item(ahead[0])
                    scores(s, 2)
                    if s > 0:
                        weigh_values(s - 1)
                    scores(s, 3)
                    if ahead:
                        item(ahead[1])
                    if s in m_step:
                        maxima(m_step[s])
                    if s in o_step:
                        turn(o_step[s])
                weigh_values(STEPS - 1)
                turn(UNITS - 1)
                pe.wait_ge(ring_read, len(ring))
                pe.wait_ge(item_read, items)

            pe.wait_ge(const_s, 2)
            for st in stages:
                kind = st[0]
                n = t_no.get(st + (0,))
                if kind in ("XT", "AT"):
                    if kind == "XT":
                        pe.wait_ge(xn_s, st[1] + 1)
                    else:
                        pe.wait_ge(att_s, UNITS - 1 + st[1])
                    for dh in range(DH):
                        turned(n + dh, [xn[:, st[1] % BLOCKS * BT + i, dh * P:(dh + 1) * P] for i in range(BT)])
                elif kind == "W_ROUTER":
                    pe.wait_ge(router_in_s, 16)
                    turned(n, [router_in[:, dh * P:(dh + 1) * P] for dh in range(DH)], E, E)
                elif kind in ("W_GATE", "W_UP"):
                    pe.wait_ge(gate_in_s if kind == "W_GATE" else up_in_s, 16)
                    src = gate_in if kind == "W_GATE" else up_in
                    turned(n, [src[:, m, dh * P:(dh + 1) * P] for m in (2 * st[1], 2 * st[1] + 1) for dh in range(DH)])
                elif kind == "W_DOWN":
                    pe.wait_ge(down_in_s, 16 * DH)
                    turned(n, [down_in[:, dh, :, m:E * F // E:CH] for m in (2 * st[1], 2 * st[1] + 1) for dh in range(DH)])
                elif kind == "W_BASIS":
                    pe.wait_ge(basis_in_s, 16 * 8)
                    turned(n, [basis_in[:, w, dh * P:(dh + 1) * P] for w in (2 * st[1], 2 * st[1] + 1) for dh in range(DH)])
                elif kind == "W_HOLO":
                    pe.wait_ge(holo_s, 2)
                    turned(n, [holo_in[:, w, hf, :, :].rearrange("p c r -> p (c r)")
                               for w in (2 * st[1], 2 * st[1] + 1) for hf in range(2)])
                elif kind == "ROUTE":
                    g = st[1]
                    l = g if g < 2 else g + 2
                    for dh in range(DH):
                        freed(pe, t_no[("XT", l, dh)])
                    freed(pe, t_no[("W_ROUTER", 0)])
                    dst = take(n)
                    product(dst[0:E, :], [lambda dh: router_hi[:, dh, :], lambda dh: router_lo[:, dh, :]],
                            xt(g % 2)).then_inc(t_full, 1)
                elif kind == "TOP":
                    freed(pe, t_no[("ROUTE", st[1], 0)])
                    turned(n, [score_t[:, i * P:(i + 1) * P] for i in range(BT)], E, E)
                elif kind == "SPREAD":
                    pe.wait_ge(spread_s, st[1] + 1)
                    turned(n, [spread[:, i, :, :].rearrange("p e r -> p (e r)") for i in range(BT)])
                elif kind == "GU":
                    _, g, m = st
                    q = g * CH + m
                    if g == 0:
                        freed(pe, t_no[("W_GATE", m // 2, 0)])
                        freed(pe, t_no[("W_UP", m // 2, 0)])
                    if q >= 2:
                        pe.wait_ge(silu_s, q - 1)
                    product(gate_b[q % 2][:, :], [lambda dh: gate_hi[:, m, dh, :], lambda dh: gate_lo[:, m, dh, :]],
                            xt(g % 2)).then_inc(gate_full, 1)
                    if q >= 2:
                        pe.wait_ge(gated_s, q - 1)
                    product(up_b[q % 2][:, :], [lambda dh: up_hi[:, m, dh, :], lambda dh: up_lo[:, m, dh, :]],
                            xt(g % 2)).then_inc(up_full, 1)
                elif kind == "DOWN":
                    _, g, i = st
                    pe.wait_ge(hid_lo_s, CH * (g + 1))
                    if g == 0:
                        for k in range(3):
                            freed(pe, t_no[("W_DOWN", k, 0)])
                    else:
                        pe.wait_ge(x_s, 2 * (g - 1) + i + 1)
                    for c in range(2):
                        at = (2 * i + c) * P
                        for m in range(CH):
                            for k, (a, b) in enumerate(THREE):
                                ins = pe.matmul(down_b[i][:, c * D:(c + 1) * D], hid[:, g % 2, a, m, at:at + P],
                                                (down_hi, down_lo)[b][:, m, :], start=(m == 0 and k == 0),
                                                stop=(m == CH - 1 and k == 2))
                    ins.then_inc(down_full, 1)
                elif kind == "RES":
                    _, w, b = st
                    for dh in range(DH):
                        freed(pe, t_no[("AT", b, dh) if w == O else ("XT", 2 + b, dh)])
                    freed(pe, t_no[("W_BASIS", w // 2, 0)])
                    dst = take(n)
                    product(dst, [lambda dh: basis_hi[:, w, dh, :], lambda dh: basis_lo[:, w, dh, :]],
                            xt(b)).then_inc(t_full, 1)
                elif kind == "QK":
                    _, w, hf, b = st
                    freed(pe, t_no[("RES", w, b, 0)])
                    freed(pe, t_no[("W_HOLO", 0, 0)])
                    dst = take(n)
                    for c, part in enumerate((holo_hi, holo_lo)):
                        ins = pe.matmul(dst, part[:, w, hf, :], res[:, w % 3, block_of(b)], start=(c == 0), stop=(c == 1))
                    ins.then_inc(t_full, 1)
                elif kind in ("V", "Y"):
                    w = V if kind == "V" else O
                    freed(pe, t_no[("RES", w, 2 * st[1] // BT, 0)])
                    freed(pe, t_no[("W_HOLO", 1, 0)])
                    dst = take(n)
                    for c in range(2):
                        at = (2 * st[1] + c) * P
                        for k, part in enumerate((holo_hi, holo_lo)):
                            ins = pe.matmul(dst[:, c * D:(c + 1) * D], res[:, w % 3, at:at + P],
                                            part[:, w, :, :].rearrange("p h o -> p (h o)"), start=(k == 0), stop=(k == 1))
                    ins.then_inc(t_full, 1)
                elif kind == "ATTENTION":
                    attention()


def kernel(L0_attn_hidden_states, L0_attn_basis_q, L0_attn_phase_q, L0_attn_amp_q, L0_attn_basis_k, L0_attn_phase_k,
           L0_attn_amp_k, L0_attn_basis_v, L0_attn_phase_v, L0_attn_amp_v, L0_attn_basis_o, L0_attn_phase_o,
           L0_attn_amp_o, L0_ffn_w_gate_router, L0_ffn_w_gate_proj, L0_ffn_w_up_proj, L0_ffn_w_down_proj):
    import concourse.bacc as bacc
    from concourse.bass_utils import run_bass_kernel_spmd

    given = {
        "x": L0_attn_hidden_states,
        "basis_q": L0_attn_basis_q, "basis_k": L0_attn_basis_k, "basis_v": L0_attn_basis_v, "basis_o": L0_attn_basis_o,
        "phase_q": L0_attn_phase_q, "phase_k": L0_attn_phase_k, "phase_v": L0_attn_phase_v, "phase_o": L0_attn_phase_o,
        "amp_q": L0_attn_amp_q, "amp_k": L0_attn_amp_k, "amp_v": L0_attn_amp_v, "amp_o": L0_attn_amp_o,
        "w_router": L0_ffn_w_gate_router, "w_gate": L0_ffn_w_gate_proj, "w_up": L0_ffn_w_up_proj,
        "w_down": L0_ffn_w_down_proj,
    }
    nc = bacc.Bacc("TRN2", target_bir_lowering=False, num_devices=1,
                   dynamic_dma_scratch_size=1024)
    arrays, dram = {}, {}
    for name, a in given.items():
        arrays[f"{name}_in"] = np.ascontiguousarray(a)
        dram[name] = nc.dram_tensor(f"{name}_in", arrays[f"{name}_in"].shape, F32, kind="ExternalInput").ap()
    out = nc.dram_tensor("out", arrays["x_in"].shape, F32, kind="ExternalOutput").ap()
    macaron_block(nc, dram["x"], [dram[f"basis_{w}"] for w in "qkvo"], [dram[f"phase_{w}"] for w in "qkvo"],
                  [dram[f"amp_{w}"] for w in "qkvo"], dram["w_router"], dram["w_gate"], dram["w_up"],
                  dram["w_down"], out)
    return run_bass_kernel_spmd(nc, [arrays], core_ids=[0]).results[0]["out"]
```

```python
from contextlib import ExitStack

import numpy as np

import concourse.bass as bass
from concourse import mybir

F32 = mybir.dt.float32
F32R = mybir.dt.float32r
U32 = mybir.dt.uint32
ALU = mybir.AluOpType
ACT = mybir.ActivationFunctionType
AX_X = mybir.AxisListType.X

P = 128
EPS = 1e-5
LN_FFN1, LN_ATT, LN_FFN2 = 0, 1, 2
Q, K, V, O = range(4)
TWO_PI = (6.28125, 0.0019350051879882812, 3.019916050448e-07)
ROUND = 12582912.0


def macaron_block(nc, x_in, w_gate, w_up, w_down, w_router, basis, phase, amp, out):
    _, S, D = x_in.shape
    E = w_router.shape[2]
    CH = w_gate.shape[1]
    HARM = basis.shape[3]
    TILES = S // P
    BLOCKS = 2
    BT = TILES // BLOCKS
    BW = S // BLOCKS
    DH = D // P
    SUB = P // E
    HD = 16
    HEADS = D // HD
    GH = 4
    GROUPS = HEADS // GH
    UNITS = GROUPS * BLOCKS
    KT = TILES
    STEPS = UNITS * KT
    ITEMS = GH * BT
    PER_STEP = ITEMS // KT
    LEAD = 10 * PER_STEP
    SCALE = 1.0 / HD ** 0.5
    assert (S, D, HARM, BW, SUB) == (1024, 256, 64, 512, 16)

    def ffn_stages(f, before, after, filler):
        g0, g1 = 2 * f, 2 * f + 1
        l1 = 4 * f + 1
        w = [[("SPLIT", name, k) for name in ("gate", "up")] if f == 0 else [] for k in range(3)]
        d = [[("SPLIT", "down", k)] if f == 0 else [] for k in range(3)]
        return (before + w[0] + [("ROUTE", g0), ("TOP", g0), ("GU", g0, 0)] + w[1] + [("LN", l1)] * (f == 0)
                + [("GU", g0, 1), ("SPREAD", g0)] + w[2] + [("GU", g0, 2)] + d[0]
                + [("GU", g0, 3), ("XT", l1), ("ROUTE", g1), ("GU", g0, 4), ("TOP", g1)] + d[1] + d[2]
                + [("GU", g0, 5), ("GU", g1, 0), ("SPREAD", g1), ("GU", g1, 1)] + [("ANGLE",)] * (f == 0)
                + [("DOWN", g0, 0), ("GU", g1, 2), ("DOWN", g0, 1)] + after[0] + [("GU", g1, 3)] + after[1]
                + [("GU", g1, 4)] + after[2] + [("GU", g1, 5), ("FLUSH", g1)] + filler
                + [("DOWN", g1, 0), ("DOWN", g1, 1)])

    def step_stages(s):
        ahead = [("ITEM", it) for it in range(LEAD + PER_STEP * s, LEAD + PER_STEP * (s + 1)) if it < UNITS * ITEMS]
        st = [("SCORES", s, 0), ("SCORES", s, 1)] + ahead[0:1] + [("SCORES", s, 2)]
        st += [("PV", s - 1)] if s > 0 else []
        st += [("PV_OUT", s // KT - 1)] if s % KT == 0 and s > 0 else []
        st += [("SCORES", s, 3)] + ahead[1:2]
        st += [("MAXIMA", (s + 2) // KT)] if (s + 2) % KT == 0 and s + 2 < STEPS else []
        st += [("TURN", s // KT - 1)] if s % KT == 1 and s > KT else []
        st += [("NORMALISE", s // KT - 1)] if s % KT == 2 and s > KT else []
        return st

    stages = ffn_stages(0, [("SPLIT", "router", 0), ("LN", 0), ("XT", 0)],
                        [[("HOLO",), ("SPLIT", "basis", 0)], [("LN", 2), ("SPLIT", "basis", 1)], [("XT", 2)]],
                        [("OWN", "projections"), ("RES", K, 0), ("RES", Q, 0), ("RES", V, 0),
                         ("SPLIT", "holo", 0), ("SPLIT", "holo", 1)])
    stages += [("LN", 3), ("QK", K, 0, 0), ("QK", Q, 0, 0), ("XT", 3), ("RES", K, 1), ("RES", Q, 1),
               ("QK", K, 0, 1), ("QK", Q, 0, 1), ("RES", V, 1), ("ONES",)] + [("V", i) for i in range(TILES // 2)]
    stages += [("QK", w, 1, b) for w in (K, Q) for b in range(2)] + [("OWN", "items")]
    for it in range(LEAD):
        stages += [("ITEM", it)] + ([("MAXIMA", 0)] if it == ITEMS else [])
    stages += [("OWN", "ring")]
    fill = {
        STEPS - 6: [("OWN", "tail"), ("AT", 0)], STEPS - 5: [("RES", O, 0)], STEPS - 4: [("Y", 0), ("Y", 1), ("LN", 4)],
        STEPS - 2: [("XT", 4)], STEPS - 1: [("ROUTE", 2), ("TOP", 2)]}
    for s in range(STEPS):
        stages += step_stages(s) + fill.get(s, [])
    stages += [("PV", STEPS - 1), ("PV_OUT", UNITS - 1), ("TURN", UNITS - 1), ("NORMALISE", UNITS - 1), ("OWN", "second FFN")]
    late = [("GU", 2, 0), ("AT", 1), ("RES", O, 1), ("GU", 2, 1), ("Y", 2), ("Y", 3), ("LN", 5), ("SPREAD", 2)]
    second = ffn_stages(1, [], [[], [], []], [])
    stages += late + [st for st in second if st not in late and st not in (("ROUTE", 2), ("TOP", 2))]

    t_no, t_bank, t_turn = {}, [], []
    banks, used = (6, 7), [0] * 8
    for st in stages:
        if st[0] == "OWN":
            banks = {"projections": (6, 7, 0, 1, 2, 3), "items": (), "ring": (), "tail": (4, 5, 6, 7), "second FFN": (6, 7)}[st[1]]
            begin = len(t_no)
        for part in range(2 if st[0] in ("XT", "AT") else st[0] in ("ROUTE", "TOP", "SPREAD", "RES", "QK", "V", "Y")):
            t_bank.append(banks[(len(t_no) - (0 if banks == (6, 7) else begin)) % len(banks)])
            t_turn.append(used[t_bank[-1]])
            used[t_bank[-1]] += 1
            t_no[st + (part,)] = len(t_no)

    r_no = {st: n for n, st in enumerate(st for st in stages if st[0] in ("SCORES", "MAXIMA", "TURN"))}
    w_no = {st: n for n, st in enumerate(st for st in stages if st[0] == "SPLIT")}

    with ExitStack() as ctx:
        def sb(name, shape, dt=F32):
            return ctx.enter_context(nc.sbuf_tensor(name, shape, dt))

        def sem(name):
            return ctx.enter_context(nc.semaphore(name))

        x = sb("x", [P, TILES, D])
        xn = sb("xn", [P, TILES, D])
        xt_hi = sb("xt_hi", [P, DH, S], F32R)
        xt_lo = sb("xt_lo", [P, DH, S], F32R)
        gate_hi = sb("gate_hi", [P, CH, DH, P], F32R)
        gate_lo = sb("gate_lo", [P, CH, DH, P], F32R)
        up_hi = sb("up_hi", [P, CH, DH, P], F32R)
        up_lo = sb("up_lo", [P, CH, DH, P], F32R)
        down_hi = sb("down_hi", [P, CH, D], F32R)
        down_lo = sb("down_lo", [P, CH, D], F32R)
        router_hi = sb("router_hi", [P, DH, E], F32R)
        router_lo = sb("router_lo", [P, DH, E], F32R)
        basis_hi = sb("basis_hi", [P, 4, DH, P], F32R)
        basis_lo = sb("basis_lo", [P, 4, DH, P], F32R)
        holo_hi = sb("holo_hi", [P, 4, 2, P], F32R)
        holo_lo = sb("holo_lo", [P, 4, 2, P], F32R)
        res = sb("res", [P, 3, S], F32R)
        v_mem = sb("v_mem", [P, KT * HEADS * 32])
        v1 = v_mem[:, :].rearrange("p (k h c) -> p k h c", k=KT, h=HEADS)
        small = 2 * D
        basis_in = v_mem[:, 0:4 * DH * HARM].rearrange("p (w h r) -> p w h r", w=4, h=DH)
        phase_in, amp_in, cos_t, cos_n = (v_mem[:, (i + 1) * small:(i + 2) * small] for i in range(4))
        router_in = sb("router_in", [P, DH, E])
        QUARTER = GH * S
        MAX_ROW = 96
        big = sb("big", [P, 4 * QUARTER], F32R)
        hid = big[:, 0:4 * CH * BW].rearrange("p (g a m t) -> p g a m t", g=2, a=2, m=CH)
        ks = [big[0:MAX_ROW + 2, i * QUARTER:(i + 1) * QUARTER].rearrange("p (j t) -> p j t", j=GH) for i in (0, 2)]
        qs = [big[0:MAX_ROW + 2, i * QUARTER:(i + 1) * QUARTER].rearrange("p (b j t) -> p b j t", b=BLOCKS, j=GH) for i in (1, 3)]
        qk_parts = big[:, 2 * QUARTER:4 * QUARTER].rearrange("p (w a h t) -> p w a h t", w=2, a=2, h=2)
        many = sb("many", [P, 3 * CH * D])
        gate_in = many[:, 0:CH * D].rearrange("p (m h f) -> p m h f", m=CH, h=DH)
        up_in = many[:, CH * D:2 * CH * D].rearrange("p (m h f) -> p m h f", m=CH, h=DH)
        down_in = many[:, 2 * CH * D:3 * CH * D].rearrange("p (m d) -> p m d", m=CH)
        holo_in = many[:, 0:4 * D].rearrange("p (w h o) -> p w h o", w=4, h=2)
        probs = many[:, 0:8 * BW].rearrange("p (n t) -> p n t", n=8)
        ident = sb("ident", [P, P])
        zeros = sb("zeros", [P, P])
        expert_no = sb("expert_no", [P, BT, E])
        minus_half = sb("minus_half", [P, BT])
        stats = sb("stats", [P, BT, 6])
        mean_var = sb("mean_var", [P, BT, 2])
        var_eps = sb("var_eps", [P, BT])
        rstd = sb("rstd", [P, BT])
        NH = 5
        feat = sb("feat", [P, NH, BW])
        route_w = sb("route_w", [P, 2, BW])
        score_t = sb("score_t", [E, BW])
        score = sb("score", [P, BT, E])
        top8 = sb("top8", [P, BT, E])
        top_no = sb("top_no", [P, BT, E], U32)
        top_nf = sb("top_nf", [P, BT, 2])
        gap = sb("gap", [P, BT, 1])
        second = sb("second", [P, BT, 1])
        prob = sb("prob", [P, 2, BT, 1])
        chosen = sb("chosen", [P, 2, BT, E])
        spread = sb("spread", [P, BT, E, SUB])
        neg_max = sb("neg_max", [P, 2, ITEMS])
        max_parts = sb("max_parts", [P, 2 * ITEMS], F32R)
        max_rows = sb("max_rows", [2 * ITEMS, P])
        pv_t = feat[:, 0, :]
        pv_q = feat[:, 1, :].rearrange("p (i j c) -> p i j c", i=BT, j=GH)
        rden = sb("rden", [P, BT, GH])
        bank = [ctx.enter_context(nc.psum_tensor(f"bank{i}", [P, 512], F32)) for i in range(4)]
        pair = [ctx.enter_context(nc.psum_tensor(f"pair{i}", [P, 2, 512], F32)) for i in range(2)]
        banks8 = [b[:, :] for b in bank] + [p[:, c, :] for p in pair for c in range(2)]
        gate_b, up_b, down_b = banks8[0:2], banks8[2:4], banks8[4:6]
        t_b = [banks8[b] for b in t_bank]
        ring_b = banks8[0:3]
        pv_b = banks8[3]
        qk_dram = nc.dram_tensor("qk_parts_dram", (2, 2, D, S), F32).ap()
        x_in_s = [sem(f"x_loaded{b}") for b in range(BLOCKS)]
        gate_in_s = [sem(f"gate_loaded{k}") for k in range(3)]
        up_in_s = [sem(f"up_loaded{k}") for k in range(3)]
        down_in_s, router_in_s = sem("down_loaded"), sem("router_loaded")
        small_in_s, holo_in_s = sem("basis_phase_amp_loaded"), sem("holo_copied")
        const_s = sem("constants_ready")
        t_full = sem("t_full")
        t_free = [sem(f"t_free{i}") for i in range(8)]
        w_hi_s, w_lo_s = sem("weight_hi_ready"), sem("weight_lo_ready")
        hi_s = sem("hi_part_ready")
        step_s = sem("vector_step")
        var_s, rstd_s, xn_s = sem("var_ready"), sem("rstd_ready"), sem("xn_ready")
        gate_full, up_full = sem("gate_full"), sem("up_full")
        tanh_s, silu_s = sem("tanh_ready"), sem("silu_ready")
        gated_s, weighed_s = sem("gated_ready"), sem("weighed_ready")
        hid_hi_s, hid_lo_s = sem("hid_hi_ready"), sem("hid_lo_ready")
        down_full, x_s = sem("down_full"), sem("x_updated")
        gap_s, second_s, spread_s = sem("gap_ready"), sem("second_ready"), sem("spread_ready")
        angle_s, sine_s, holo_s = sem("angle_ready"), sem("sine_ready"), sem("holo_ready")
        qk_out_s = [sem(f"qk_stored{i}") for i in range(4)]
        ones_s, zero_rows_s = sem("ones_ready"), sem("zero_rows_ready")
        k_stack_s = [sem("k_stack_loaded0"), sem("k_stack_loaded1")]
        q_stack_s = [[sem(f"q_stack_loaded{i}{b}") for b in range(BLOCKS)] for i in range(2)]
        item_full, item_read = sem("item_full"), sem("item_read")
        max_parts_s, max_in_s = sem("max_parts_ready"), sem("max_rows_placed")
        ring_full, ring_read = sem("ring_full"), sem("ring_read")
        pv_s, pv_read = sem("pv_steps_done"), sem("pv_read")
        att_s = sem("attention_unit_ready")
        out_s = sem("out_stored")

        x_tok = x_in.rearrange("a (p i) d -> (a p) i d", p=P)
        out_tok = out.rearrange("a (p i) d -> (a p) i d", p=P)
        def freed(eng, n):
            eng.wait_ge(t_free[t_bank[n]], t_turn[n] + 1)

        def bank_uses(banks_wanted, before):
            first = stages.index(before)
            uses = [t_no[st + (part,)] for st in stages[:first] for part in range(2) if st + (part,) in t_no]
            return [(b, sum(t_bank[n] == b for n in uses)) for b in banks_wanted]

        def lo_ready(eng, name, k):
            eng.wait_ge(w_lo_s, w_no[("SPLIT", name, k)] + 1)

        def block_of(b):
            return slice(b * BW, (b + 1) * BW)

        def tiles_of(b):
            return slice(b * BT, (b + 1) * BT)

        def split_of(st, part):
            if st[0] in ("XT", "AT"):
                b = st[1] % BLOCKS
                return xt_hi[:, part, block_of(b)], xt_lo[:, part, block_of(b)]
            _, w, hf, b = st
            return qk_parts[:, w, 0, hf, block_of(b)], qk_parts[:, w, 1, hf, block_of(b)]

        def weights_of(name, k):
            two = slice(2 * k, 2 * k + 2)
            if name == "router":
                return router_in[:, :, :], router_hi[:, :, :], router_lo[:, :, :]
            if name == "basis":
                src = basis_in[:, two, :, :].rearrange("p w h r -> p (w h) r").unsqueeze(2).broadcast_to([P, 2 * DH, 2, HARM])
                return (src, *(t[:, two, :, :].rearrange("p w h (c r) -> p (w h) c r", c=2) for t in (basis_hi, basis_lo)))
            if name == "holo":
                return holo_in[:, two, :, :], holo_hi[:, two, :, :], holo_lo[:, two, :, :]
            if name == "down":
                return down_in[:, two, :], down_hi[:, two, :], down_lo[:, two, :]
            src, hi, lo = {"gate": (gate_in, gate_hi, gate_lo), "up": (up_in, up_hi, up_lo)}[name]
            return src[:, two, :, :], hi[:, two, :, :], lo[:, two, :, :]

        def weights_in(eng, name, k):
            if name in ("gate", "up"):
                eng.wait_ge((gate_in_s if name == "gate" else up_in_s)[k], 16)
            elif name == "holo":
                eng.wait_ge(holo_in_s, 16 * 4)
            else:
                eng.wait_ge({"router": router_in_s, "down": down_in_s, "basis": small_in_s}[name],
                            16 * {"router": 1, "down": 1, "basis": 3}[name])

        def seen_as(bank_ap, like):
            dims = list(like.shape)[1:]
            flat = bank_ap[:, 0:int(np.prod(dims))]
            if len(dims) == 1:
                return flat
            if len(dims) == 2:
                return flat.rearrange("p (a b) -> p a b", a=dims[0])
            return flat.rearrange("p (a b c) -> p a b c", a=dims[0], b=dims[1])

        block = ctx.enter_context(nc.Block())

        @block.sync
        def _(sp):
            sp.dma_start(x[:, 0:BT, :], x_tok[:, 0:BT, :]).then_inc(x_in_s[0], 16)
            sp.dma_start(router_in[:, :, :], w_router).then_inc(router_in_s, 16)
            for k in range(3):
                two = slice(2 * k, 2 * k + 2)
                sp.dma_start(gate_in[:, two, :, :], w_gate[:, two, :, :]).then_inc(gate_in_s[k], 16)
                sp.dma_start(up_in[:, two, :, :], w_up[:, two, :, :]).then_inc(up_in_s[k], 16)
                if k == 0:
                    sp.dma_start(x[:, BT:TILES, :], x_tok[:, BT:TILES, :]).then_inc(x_in_s[1], 16)
            sp.dma_start(down_in, w_down).then_inc(down_in_s, 16)
            sp.dma_start(basis_in, basis).then_inc(small_in_s, 16)
            sp.dma_start(phase_in, phase.rearrange("p w o -> p (w o)")).then_inc(small_in_s, 16)
            sp.dma_start(amp_in, amp.rearrange("p w o -> p (w o)")).then_inc(small_in_s, 16)
            sp.wait_ge(holo_s, 1)
            lo_ready(sp, "gate", 2)
            for pr in range(2):
                for c in range(2):
                    sp.dma_start(holo_in[c * HARM:(c + 1) * HARM, 2 * pr:2 * pr + 2, :, :],
                                 cos_t[pr * HARM:(pr + 1) * HARM, :].rearrange("p (w h o) -> p w h o", w=2, h=2)
                                 ).then_inc(holo_in_s, 16)

            def store_parts(hg):
                hf, at = hg // 2, hg % 2 * GH * HD
                for w in (K, Q):
                    for b in range(BLOCKS):
                        freed(sp, t_no[("QK", w, hf, b, 0)])
                    sp.dma_start(qk_dram[w][:, hf * P + at:hf * P + at + GH * HD, :].rearrange("a p t -> p a t"),
                                 qk_parts[at:at + GH * HD, w, :, hf, :].bitcast(F32)).then_inc(qk_out_s[hg], 16)

            def load_stacks(hg):
                sp.wait_ge(qk_out_s[hg], 32)
                if hg == 1:
                    for i in (2, 3):
                        sp.wait_ge(qk_out_s[i], 32)
                if hg >= 2:
                    sp.wait_ge(pv_s, 2 * KT * (hg - 1))
                rows = slice(hg * GH * HD, (hg + 1) * GH * HD)
                for c, part in enumerate((0, 0, 1, 1)):
                    sp.dma_start(ks[hg % 2][c * HD:(c + 1) * HD, :, :].bitcast(F32),
                                 qk_dram[K][part, rows, :].rearrange("(j d) t -> d j t", j=GH)
                                 ).then_inc(k_stack_s[hg % 2], 16)
                for b in range(BLOCKS):
                    for c, part in enumerate((0, 1, 0, 1)):
                        sp.dma_start(qs[hg % 2][c * HD:(c + 1) * HD, b, :, :].bitcast(F32),
                                     qk_dram[Q][part, rows, block_of(b)].rearrange("(j d) t -> d j t", j=GH)
                                     ).then_inc(q_stack_s[hg % 2][b], 16)

            store_parts(0)
            load_stacks(0)
            for hg in range(1, GROUPS):
                store_parts(hg)
            load_stacks(1)
            for u in range(UNITS):
                hg, b = u // BLOCKS, u % BLOCKS
                sp.wait_ge(ring_read, r_no[("MAXIMA", u)] + 1)
                for part in range(2):
                    sp.dma_start(qs[hg % 2][MAX_ROW + part:MAX_ROW + part + 1, b, :, :].bitcast(F32)
                                 .rearrange("o j (i c) -> o (j i) c", c=P),
                                 max_rows[part * ITEMS:(part + 1) * ITEMS, :]).then_inc(max_in_s, 16)
                if u in (2, 4):
                    load_stacks(u // 2 + 1)
            for b in range(BLOCKS):
                sp.wait_ge(x_s, 2 * BLOCKS + 2 * (b + 1))
                sp.dma_start(out_tok[:, tiles_of(b), :], x[:, tiles_of(b), :]).then_inc(out_s, 16)
            sp.wait_ge(out_s, 16 * BLOCKS)

        @block.gpsimd
        def _(pool):
            pool.memset(zeros[:, :], 0.0).then_inc(const_s, 1)
            pool.wait_ge(const_s, 1)
            pool.affine_select(out=ident[:, :], in_=zeros[:, :], compare_op=ALU.not_equal, fill=1.0, base=0,
                               pattern=[[-1, P]], channel_multiplier=1).then_inc(const_s, 1)
            pool.memset(minus_half[:, :], -0.5).then_inc(const_s, 1)
            for e in range(E):
                pool.memset(expert_no[:, :, e:e + 1], float(e)).then_inc(const_s, 1)

            def split_lo(st):
                src, hi, lo = weights_of(*st[1:])
                pool.wait_ge(w_hi_s, w_no[st] + 1)
                pool.tensor_tensor(lo, src, hi.bitcast(F32), ALU.subtract).then_inc(w_lo_s, 1)

            def weigh(n):
                g, m = n // CH, n % CH
                pool.wait_ge(gated_s, n + 1)
                if m == 0:
                    freed(pool, t_no[("SPREAD", g, 0)])
                pool.tensor_tensor(feat[:, n % NH, :], feat[:, n % NH, :], route_w[:, g % 2, :],
                                   ALU.mult).then_inc(weighed_s, 1)

            for st in stages:
                if st[0] == "LN":
                    l = st[1]
                    pool.wait_ge(var_s, l + 1)
                    if l == 0:
                        pool.wait_ge(const_s, 3)
                    else:
                        pool.wait_ge(xn_s, l)
                    pool.tensor_tensor(rstd[:, :], var_eps[:, :], minus_half[:, :], ALU.pow).then_inc(rstd_s, 1)
                elif st[0] == "SPLIT":
                    split_lo(st)
                elif st[0] == "GU":
                    n = st[1] * CH + st[2]
                    if n % (2 * CH):
                        weigh(n - 1)
                elif st[0] == "FLUSH":
                    weigh((st[1] + 1) * CH - 1)
                elif st[0] == "ONES":
                    lo_ready(pool, "basis", 1)
                    pool.wait_ge(holo_in_s, 16 * 4)
                    pool.memset(v1[:, :, :, HD:32], 1.0).then_inc(ones_s, 1)
                elif st == ("OWN", "items"):
                    pool.wait_ge(ones_s, 1)
                    pool.wait_ge(x_s, 4)
                    for hg in range(GROUPS):
                        if hg == 1:
                            for i in range(GROUPS):
                                pool.wait_ge(qk_out_s[i], 32)
                        if hg < 2:
                            pool.memset(ks[hg][MAX_ROW:MAX_ROW + 2, :, :].bitcast(F32), 1.0).then_inc(ones_s, 1)
                            pool.wait_ge(ones_s, 3 * hg + 2)
                            pool.memset(ks[hg][64:MAX_ROW, :, :].bitcast(F32), 0.0).then_inc(ones_s, 1)
                            pool.wait_ge(ones_s, 3 * hg + 3)
                            pool.memset(qs[hg][64:MAX_ROW, :, :, :].bitcast(F32), 0.0).then_inc(ones_s, 1)
                            pool.wait_ge(ones_s, 3 * hg + 4)
                        else:
                            pool.wait_ge(pv_s, 2 * KT * (hg - 1))
                        pool.memset(qs[hg % 2][MAX_ROW:MAX_ROW + 2, :, :, :].bitcast(F32), 0.0).then_inc(zero_rows_s, 1)
                        pool.wait_ge(zero_rows_s, hg + 1)

        @block.scalar
        def _(act):
            def hid_hi(n):
                g, m = n // CH, n % CH
                act.wait_ge(weighed_s, n + 1)
                act.copy(hid[:, g % 2, 0, m, :], feat[:, n % NH, :]).then_inc(hid_hi_s, 1)

            for st in stages:
                kind = st[0]
                if kind == "SPLIT":
                    src, hi, _ = weights_of(*st[1:])
                    weights_in(act, *st[1:])
                    act.copy(hi, src).then_inc(w_hi_s, 1)
                elif kind in ("XT", "AT", "QK"):
                    for part in range(2 if kind in ("XT", "AT") else 1):
                        n = t_no[st + (part,)]
                        hi, _ = split_of(st, part)
                        act.wait_ge(t_full, n + 1)
                        act.copy(hi, seen_as(t_b[n], hi)).then_inc(hi_s, 1)
                elif kind == "RES":
                    _, w, b = st
                    n = t_no[st + (0,)]
                    act.wait_ge(t_full, n + 1)
                    act.copy(res[:, w % 3, block_of(b)], t_b[n]).then_inc(hi_s, 1)
                elif kind == "ROUTE":
                    n = t_no[st + (0,)]
                    act.wait_ge(t_full, n + 1)
                    act.copy(score_t[:, :], t_b[n][0:E, :]).then_inc(t_free[t_bank[n]], 1)
                elif kind == "TOP":
                    act.wait_ge(gap_s, st[1] + 1)
                    act.activation(second[:, :, :], gap[:, :, :], ACT.Exp).then_inc(second_s, 1)
                elif kind == "SPREAD":
                    n = t_no[st + (0,)]
                    if st[1] >= 2:
                        act.wait_ge(weighed_s, CH * (st[1] - 1))
                    act.wait_ge(t_full, n + 1)
                    act.copy(route_w[:, st[1] % 2, :], t_b[n]).then_inc(t_free[t_bank[n]], 1)
                elif kind == "GU":
                    _, g, m = st
                    n = g * CH + m
                    act.wait_ge(gate_full, n + 1)
                    if n >= NH:
                        act.wait_ge(hid_lo_s, n - NH + 1)
                    act.activation(feat[:, n % NH, :], gate_b[n % 2][:, :], ACT.Tanh, scale=0.5).then_inc(tanh_s, 1)
                    if n > n // (2 * CH) * 2 * CH + 1:
                        hid_hi(n - 2)
                elif kind == "FLUSH":
                    hid_hi((st[1] + 1) * CH - 2)
                    hid_hi((st[1] + 1) * CH - 1)
                elif kind == "ANGLE":
                    act.wait_ge(angle_s, 1)
                    act.activation(cos_n, cos_t, ACT.Sin, scale=0.5).then_inc(sine_s, 1)
                elif kind == "V":
                    n = t_no[st + (0,)]
                    act.wait_ge(t_full, n + 1)
                    act.copy(v1[:, 2 * st[1]:2 * st[1] + 2, :, 0:HD],
                             t_b[n].rearrange("p (i h c) -> p i h c", i=2, h=HEADS)).then_inc(t_free[t_bank[n]], 1)
                elif kind == "MAXIMA":
                    act.wait_ge(ring_full, r_no[st] + 1)
                    if st[1] >= 1:
                        act.wait_ge(max_in_s, 32 * st[1])
                    act.copy(max_rows[:, :], ring_b[r_no[st] % 3][0:2 * ITEMS, 0:P]).then_inc(ring_read, 1)
                elif kind == "SCORES":
                    _, s, j = st
                    act.wait_ge(ring_full, r_no[st] + 1)
                    if s >= 2:
                        act.wait_ge(pv_s, s - 1)
                    act.activation(probs[:, (GH * s + j) % 8, :], ring_b[r_no[st] % 3], ACT.Exp,
                                   scale=SCALE).then_inc(ring_read, 1)
                elif kind == "PV_OUT":
                    act.wait_ge(pv_s, KT * (st[1] + 1))
                    act.copy(pv_t, pv_b).then_inc(pv_read, 1)
                elif kind == "TURN":
                    act.wait_ge(ring_full, r_no[st] + 1)
                    if st[1] >= 1:
                        act.wait_ge(att_s, st[1])
                    act.copy(pv_q, ring_b[r_no[st] % 3].rearrange("p (i j c) -> p i j c", i=BT, j=GH)
                             ).then_inc(ring_read, 1)

        @block.vector
        def _(dve):
            steps = [0]

            def link(ins):
                steps[0] += 1
                ins.then_inc(step_s, 1)
                dve.wait_ge(step_s, steps[0])

            hi_no = [0]

            def lo_part(n, lo, hi, src):
                hi_no[0] += 1
                dve.wait_ge(hi_s, hi_no[0])
                dve.tensor_tensor(lo, src, hi.bitcast(F32), ALU.subtract).then_inc(t_free[t_bank[n]], 1)

            def layer_norm(l):
                b = l % BLOCKS
                if l < 2:
                    dve.wait_ge(x_in_s[b], 16)
                elif l < 4:
                    dve.wait_ge(x_s, 2 * (b + 1))
                else:
                    freed(dve, t_no[("Y", 2 * b + 1, 0)])
                for i in range(BT):
                    ins = dve.bn_stats(stats[:, i, :], x[:, b * BT + i, :])
                link(ins)
                for i in range(BT):
                    ins = dve.bn_aggr(mean_var[:, i, :], stats[:, i, :])
                link(ins)
                dve.tensor_scalar(var_eps[:, :], mean_var[:, :, 1], EPS, None, ALU.add).then_inc(var_s, 1)
                dve.wait_ge(rstd_s, l + 1)
                for i in range(BT):
                    ins = dve.tensor_scalar(xn[:, b * BT + i, :], x[:, b * BT + i, :], mean_var[:, i, 0:1],
                                            rstd[:, i:i + 1], ALU.subtract, ALU.mult)
                ins.then_inc(xn_s, 1)

            def route(g, n):
                dve.wait_ge(t_full, n + 1)
                if g == 0:
                    dve.wait_ge(const_s, 3 + E)
                ins = dve.tensor_copy(score[:, :, :], t_b[n][:, 0:BT * E].rearrange("p (i e) -> p i e", i=BT))
                ins.then_inc(t_free[t_bank[n]], 1)
                freed(dve, n)
                for i in range(BT):
                    ins = dve.max(top8[:, i, :], score[:, i, :])
                link(ins)
                for i in range(BT):
                    ins = dve.max_index(top_no[:, i, :], top8[:, i, :], score[:, i, :])
                link(ins)
                dve.tensor_tensor(gap[:, :, :], top8[:, :, 1:2], top8[:, :, 0:1], ALU.subtract).then_inc(gap_s, 1)
                link(dve.tensor_copy(top_nf[:, :, :], top_no[:, :, 0:2]))
                for c in range(2):
                    ins = dve.tensor_tensor(chosen[:, c, :, :], expert_no[:, :, :],
                                            top_nf[:, :, c:c + 1].broadcast_to([P, BT, E]), ALU.is_equal)
                link(ins)
                dve.wait_ge(second_s, g + 1)
                link(dve.tensor_scalar(prob[:, 1, :, :], second[:, :, :], 4.0, 4.0, ALU.mult, ALU.add))
                link(dve.reciprocal(prob[:, 0, :, :], prob[:, 1, :, :]))
                link(dve.tensor_tensor(prob[:, 1, :, :], prob[:, 0, :, :], second[:, :, :], ALU.mult))
                for c in range(2):
                    ins = dve.tensor_tensor(chosen[:, c, :, :], chosen[:, c, :, :],
                                            prob[:, c, :, :].broadcast_to([P, BT, E]), ALU.mult)
                link(ins)
                link(dve.tensor_tensor(chosen[:, 0, :, :], chosen[:, 0, :, :], chosen[:, 1, :, :], ALU.add))
                dve.tensor_copy(spread[:, :, :, :].rearrange("p i e r -> p (i e) r"),
                                chosen[:, 0, :, :].rearrange("p i e -> p (i e)").unsqueeze(2)
                                .broadcast_to([P, BT * E, SUB])).then_inc(spread_s, 1)

            def normalise(u):
                hg, b = u // BLOCKS, u % BLOCKS
                dve.wait_ge(ring_read, r_no[("TURN", u)] + 1)
                link(dve.reciprocal(rden[:, :, :], pv_q[:, :, :, HD]))
                dve.tensor_tensor(xn[:, tiles_of(b), hg * GH * HD:(hg + 1) * GH * HD]
                                  .rearrange("p i (j c) -> p i j c", j=GH),
                                  pv_q[:, :, :, 0:HD],
                                  rden[:, :, :].unsqueeze(3).broadcast_to([P, BT, GH, HD]), ALU.mult).then_inc(att_s, 1)

            def hid_lo(n):
                g, m = n // CH, n % CH
                dve.wait_ge(hid_hi_s, n + 1)
                dve.tensor_tensor(hid[:, g % 2, 1, m, :], feat[:, n % NH, :],
                                  hid[:, g % 2, 0, m, :].bitcast(F32), ALU.subtract).then_inc(hid_lo_s, 1)

            for st in stages:
                kind = st[0]
                if kind == "LN":
                    layer_norm(st[1])
                elif kind in ("XT", "AT", "QK"):
                    for part in range(2 if kind in ("XT", "AT") else 1):
                        n = t_no[st + (part,)]
                        hi, lo = split_of(st, part)
                        lo_part(n, lo, hi, seen_as(t_b[n], hi))
                elif kind == "RES":
                    _, w, b = st
                    n = t_no[st + (0,)]
                    both = res[HARM:2 * HARM, w % 3, block_of(b)]
                    lo_part(n, both, both, t_b[n][HARM:2 * HARM, :])
                elif kind == "TOP":
                    route(st[1], t_no[st + (0,)])
                elif kind == "GU":
                    _, g, m = st
                    n = g * CH + m
                    dve.wait_ge(tanh_s, n + 1)
                    dve.scalar_tensor_tensor(out=feat[:, n % NH, :], in0=feat[:, n % NH, :], scalar=1.0,
                                             in1=gate_b[n % 2][:, :], op0=ALU.add, op1=ALU.mult).then_inc(silu_s, 1)
                    dve.wait_ge(silu_s, n + 1)
                    dve.wait_ge(up_full, n + 1)
                    dve.tensor_tensor(feat[:, n % NH, :], feat[:, n % NH, :], up_b[n % 2][:, :],
                                      ALU.mult).then_inc(gated_s, 1)
                    if n > n // (2 * CH) * 2 * CH + 1:
                        hid_lo(n - 2)
                elif kind == "FLUSH":
                    hid_lo((st[1] + 1) * CH - 2)
                    hid_lo((st[1] + 1) * CH - 1)
                elif kind == "DOWN":
                    _, g, i = st
                    dve.wait_ge(down_full, 2 * g + i + 1)
                    tiles = slice(g % 2 * BT + 2 * i, g % 2 * BT + 2 * i + 2)
                    dve.tensor_tensor(x[:, tiles, :], x[:, tiles, :],
                                      down_b[i].rearrange("p (a d) -> p a d", a=2), ALU.add).then_inc(x_s, 1)
                elif kind == "Y":
                    n = t_no[st + (0,)]
                    tiles = slice(2 * st[1], 2 * st[1] + 2)
                    dve.wait_ge(t_full, n + 1)
                    dve.tensor_tensor(x[:, tiles, :], x[:, tiles, :],
                                      t_b[n].rearrange("p (a d) -> p a d", a=2), ALU.add).then_inc(t_free[t_bank[n]], 1)
                elif kind == "ANGLE":
                    ph = phase_in
                    dve.wait_ge(small_in_s, 16 * 3)
                    link(dve.tensor_scalar(cos_n, ph, 1.0 / (2.0 * np.pi), ROUND, ALU.mult, ALU.add))
                    link(dve.tensor_scalar(cos_n, cos_n, ROUND, None, ALU.subtract))
                    link(dve.scalar_tensor_tensor(out=cos_t, in0=cos_n, scalar=-TWO_PI[0], in1=ph,
                                                  op0=ALU.mult, op1=ALU.add))
                    link(dve.scalar_tensor_tensor(out=cos_t, in0=cos_n, scalar=-TWO_PI[1], in1=cos_t,
                                                  op0=ALU.mult, op1=ALU.add))
                    dve.scalar_tensor_tensor(out=cos_t, in0=cos_n, scalar=-TWO_PI[2], in1=cos_t,
                                             op0=ALU.mult, op1=ALU.add).then_inc(angle_s, 1)
                elif kind == "HOLO":
                    dve.wait_ge(sine_s, 1)
                    link(dve.tensor_tensor(cos_t, cos_n, cos_n, ALU.mult))
                    link(dve.tensor_scalar(cos_n, cos_t, -2.0, 1.0, ALU.mult, ALU.add))
                    dve.tensor_tensor(cos_t, cos_n, amp_in, ALU.mult).then_inc(holo_s, 1)
                elif kind == "ITEM":
                    u, i = st[1] // ITEMS, st[1] % ITEMS
                    dve.wait_ge(item_full, st[1] + 1)
                    dve.tensor_reduce(neg_max[:, u % 2, i:i + 1], pair[st[1] % 2][:, :, :].rearrange("p a b -> p (a b)"),
                                      AX_X, ALU.max, negate=True).then_inc(item_read, 1)
                    if i == ITEMS - 1:
                        dve.wait_ge(item_read, st[1] + 1)
                        if u >= 1:
                            dve.wait_ge(ring_full, r_no[("MAXIMA", u - 1)] + 1)
                        link(dve.tensor_copy(max_parts[:, 0:ITEMS], neg_max[:, u % 2, :]))
                        dve.tensor_tensor(max_parts[:, ITEMS:2 * ITEMS], neg_max[:, u % 2, :],
                                          max_parts[:, 0:ITEMS].bitcast(F32), ALU.subtract).then_inc(max_parts_s, 1)
                elif kind == "NORMALISE":
                    normalise(st[1])

        @block.tensor
        def _(pe):
            THREE = ((0, 0), (0, 1), (1, 0))

            def take(n):
                if t_turn[n] > 0:
                    pe.wait_ge(t_free[t_bank[n]], t_turn[n])
                elif t_bank[n] < 4:
                    pe.wait_ge(silu_s, 2 * CH)
                    pe.wait_ge(gated_s, 2 * CH)
                return t_b[n]

            def product(dst, stationary, moving, last_of_group=True):
                for dh in range(DH):
                    for c, (a, b) in enumerate(THREE):
                        ins = pe.matmul(dst, stationary[a](dh), moving[b](dh),
                                        start=(dh == 0 and c == 0), stop=(dh == DH - 1 and c == 2))
                return ins

            def xt(b):
                return [lambda dh: xt_hi[:, dh, block_of(b)], lambda dh: xt_lo[:, dh, block_of(b)]]

            def turned(n, sources, width=P, rows=P):
                dst = take(n)
                for c, src in enumerate(sources):
                    ins = pe.transpose(dst[:, c * width:(c + 1) * width], src, ident[0:rows, 0:rows])
                ins.then_inc(t_full, 1)

            def item(it):
                u, i = it // ITEMS, it % ITEMS
                hg, b = u // BLOCKS, u % BLOCKS
                j, tile = i // BT, i % BT
                if b == 0 and i == 0:
                    pe.wait_ge(k_stack_s[hg % 2], 4 * 16 * (hg // 2 + 1))
                    pe.wait_ge(zero_rows_s, hg + 1)
                if i == 0:
                    pe.wait_ge(q_stack_s[hg % 2][b], 4 * 16 * (hg // 2 + 1))
                if it >= 2:
                    pe.wait_ge(item_read, it - 1)
                for c in range(2):
                    ins = pe.matmul(pair[it % 2][:, c, :], qs[hg % 2][:, b, j, tile * P:(tile + 1) * P],
                                    ks[hg % 2][:, j, c * BW:(c + 1) * BW], start=True, stop=True)
                ins.then_inc(item_full, 1)

            def ring_take(use):
                n = r_no[use]
                if n >= 3:
                    pe.wait_ge(ring_read, n - 2)
                return ring_b[n % 3]

            def maxima(u):
                pe.wait_ge(max_parts_s, u + 1)
                dst = ring_take(("MAXIMA", u))
                pe.transpose(dst[0:2 * ITEMS, 0:P], max_parts[:, :].bitcast(F32), ident[:, :]).then_inc(ring_full, 1)

            def scores(s, j):
                u, kt = s // KT, s % KT
                hg, b = u // BLOCKS, u % BLOCKS
                if kt == 0 and j == 0:
                    pe.wait_ge(max_in_s, 32 * (u + 1))
                dst = ring_take(("SCORES", s, j))
                pe.matmul(dst[:, :], ks[hg % 2][:, j, kt * P:(kt + 1) * P], qs[hg % 2][:, b, j, :],
                          start=True, stop=True).then_inc(ring_full, 1)

            def weigh_values(s):
                u, kt = s // KT, s % KT
                if s == 0:
                    for i in (TILES // 2 - 2, TILES // 2 - 1):
                        freed(pe, t_no[("V", i, 0)])
                    pe.wait_ge(ones_s, 1)
                if kt == 0 and u >= 1:
                    pe.wait_ge(pv_read, u)
                pe.wait_ge(ring_read, r_no[("SCORES", s, GH - 1)] + 1)
                for j in range(GH):
                    ins = pe.matmul(pv_b[32 * j:32 * j + 32, :], v1[:, kt, u // BLOCKS * GH + j, :],
                                    probs[:, (GH * s + j) % 8, :], start=(kt == 0), stop=(kt == KT - 1))
                ins.then_inc(pv_s, 1)

            def turn(u):
                pe.wait_ge(pv_read, u + 1)
                dst = ring_take(("TURN", u))
                for i in range(BT):
                    ins = pe.transpose(dst[:, i * P:(i + 1) * P], pv_t[:, i * P:(i + 1) * P], ident[:, :])
                ins.then_inc(ring_full, 1)

            def own(phase):
                of = {"projections": (), "items": (6, 7), "ring": (0, 1, 2, 3), "tail": (), "second FFN": (4, 5)}[phase]
                for b, uses in bank_uses(of, ("OWN", phase)):
                    if uses:
                        pe.wait_ge(t_free[b], uses)
                if phase == "items":
                    pe.wait_ge(x_s, 4)
                elif phase == "tail":
                    pe.wait_ge(item_read, UNITS * ITEMS)
                elif phase == "second FFN":
                    pe.wait_ge(ring_read, len(r_no))
                    pe.wait_ge(pv_read, UNITS)

            pe.wait_ge(const_s, 2)
            for st in stages:
                kind = st[0]
                n = t_no.get(st + (0,))
                if kind in ("XT", "AT"):
                    if kind == "XT":
                        pe.wait_ge(xn_s, st[1] + 1)
                    else:
                        pe.wait_ge(att_s, UNITS - 1 + st[1])
                    for dh in range(DH):
                        turned(n + dh, [xn[:, st[1] % BLOCKS * BT + i, dh * P:(dh + 1) * P] for i in range(BT)])
                elif kind == "ROUTE":
                    g = st[1]
                    l = g if g < 2 else g + 2
                    for dh in range(DH):
                        freed(pe, t_no[("XT", l, dh)])
                    lo_ready(pe, "router", 0)
                    dst = take(n)
                    product(dst[0:E, :], [lambda dh: router_hi[:, dh, :], lambda dh: router_lo[:, dh, :]],
                            xt(g % 2)).then_inc(t_full, 1)
                elif kind == "TOP":
                    freed(pe, t_no[("ROUTE", st[1], 0)])
                    turned(n, [score_t[:, i * P:(i + 1) * P] for i in range(BT)], E, E)
                elif kind == "SPREAD":
                    pe.wait_ge(spread_s, st[1] + 1)
                    turned(n, [spread[:, i, :, :].rearrange("p e r -> p (e r)") for i in range(BT)])
                elif kind == "GU":
                    _, g, m = st
                    q = g * CH + m
                    if g == 0:
                        lo_ready(pe, "gate", m // 2)
                        lo_ready(pe, "up", m // 2)
                    if q >= 2:
                        pe.wait_ge(silu_s, q - 1)
                    product(gate_b[q % 2][:, :], [lambda dh: gate_hi[:, m, dh, :], lambda dh: gate_lo[:, m, dh, :]],
                            xt(g % 2)).then_inc(gate_full, 1)
                    if q >= 2:
                        pe.wait_ge(gated_s, q - 1)
                    product(up_b[q % 2][:, :], [lambda dh: up_hi[:, m, dh, :], lambda dh: up_lo[:, m, dh, :]],
                            xt(g % 2)).then_inc(up_full, 1)
                elif kind == "DOWN":
                    _, g, i = st
                    if g == 0:
                        lo_ready(pe, "down", 2)
                    else:
                        pe.wait_ge(x_s, 2 * (g - 1) + i + 1)
                    for c in range(2):
                        at = (2 * i + c) * P
                        for m in range(CH):
                            if i == 0 and c == 0:
                                pe.wait_ge(hid_lo_s, CH * g + m + 1)
                            for k, (a, b) in enumerate(THREE):
                                ins = pe.matmul(down_b[i][:, c * D:(c + 1) * D], hid[:, g % 2, a, m, at:at + P],
                                                (down_hi, down_lo)[b][:, m, :], start=(m == 0 and k == 0),
                                                stop=(m == CH - 1 and k == 2))
                    ins.then_inc(down_full, 1)
                elif kind == "RES":
                    _, w, b = st
                    for dh in range(DH):
                        freed(pe, t_no[("AT", b, dh) if w == O else ("XT", 2 + b, dh)])
                    lo_ready(pe, "basis", w // 2)
                    dst = take(n)
                    product(dst, [lambda dh: basis_hi[:, w, dh, :], lambda dh: basis_lo[:, w, dh, :]],
                            xt(b)).then_inc(t_full, 1)
                elif kind == "QK":
                    _, w, hf, b = st
                    freed(pe, t_no[("RES", w, b, 0)])
                    lo_ready(pe, "holo", 0)
                    dst = take(n)
                    for c, part in enumerate((holo_hi, holo_lo)):
                        ins = pe.matmul(dst, part[:, w, hf, :], res[:, w % 3, block_of(b)], start=(c == 0), stop=(c == 1))
                    ins.then_inc(t_full, 1)
                elif kind in ("V", "Y"):
                    w = V if kind == "V" else O
                    freed(pe, t_no[("RES", w, 2 * st[1] // BT, 0)])
                    lo_ready(pe, "holo", 1)
                    dst = take(n)
                    for c in range(2):
                        at = (2 * st[1] + c) * P
                        for k, part in enumerate((holo_hi, holo_lo)):
                            ins = pe.matmul(dst[:, c * D:(c + 1) * D], res[:, w % 3, at:at + P],
                                            part[:, w, :, :].rearrange("p h o -> p (h o)"), start=(k == 0), stop=(k == 1))
                    ins.then_inc(t_full, 1)
                elif kind == "ITEM":
                    item(st[1])
                elif kind == "MAXIMA":
                    maxima(st[1])
                elif kind == "SCORES":
                    scores(*st[1:])
                elif kind == "PV":
                    weigh_values(st[1])
                elif kind == "TURN":
                    turn(st[1])
                elif kind == "OWN":
                    own(st[1])


def kernel(L0_attn_hidden_states, L0_attn_basis_q, L0_attn_phase_q, L0_attn_amp_q, L0_attn_basis_k, L0_attn_phase_k,
           L0_attn_amp_k, L0_attn_basis_v, L0_attn_phase_v, L0_attn_amp_v, L0_attn_basis_o, L0_attn_phase_o,
           L0_attn_amp_o, L0_ffn_w_gate_router, L0_ffn_w_gate_proj, L0_ffn_w_up_proj, L0_ffn_w_down_proj):
    import concourse.bacc as bacc
    from concourse.bass_utils import run_bass_kernel_spmd

    w_gate, w_up = (w.reshape(128, 6, 2, 128).transpose(3, 1, 2, 0) for w in (L0_ffn_w_gate_proj, L0_ffn_w_up_proj))
    basis = np.stack([L0_attn_basis_q, L0_attn_basis_k, L0_attn_basis_v, L0_attn_basis_o])
    phase = np.stack([L0_attn_phase_q, L0_attn_phase_k, L0_attn_phase_v, L0_attn_phase_o])
    amp = np.stack([L0_attn_amp_q, L0_attn_amp_k, L0_attn_amp_v, L0_attn_amp_o])
    given = {
        "x": L0_attn_hidden_states,
        "w_gate": w_gate, "w_up": w_up,
        "w_down": L0_ffn_w_down_proj.transpose(0, 2, 1).reshape(128, 6, 256),
        "w_router": L0_ffn_w_gate_router.reshape(8, 2, 128).transpose(2, 1, 0),
        "basis": basis.reshape(4, 64, 2, 128).transpose(3, 0, 2, 1),
        "phase": phase.reshape(2, 2, 256, 64).transpose(0, 3, 1, 2).reshape(128, 2, 256),
        "amp": amp.reshape(2, 2, 256, 64).transpose(0, 3, 1, 2).reshape(128, 2, 256),
    }
    nc = bacc.Bacc("TRN2", target_bir_lowering=False, num_devices=1,
                   dynamic_dma_scratch_size=1024)
    arrays, dram = {}, {}
    for name, a in given.items():
        arrays[f"{name}_in"] = np.ascontiguousarray(a)
        dram[name] = nc.dram_tensor(f"{name}_in", arrays[f"{name}_in"].shape, F32, kind="ExternalInput").ap()
    out = nc.dram_tensor("out", arrays["x_in"].shape, F32, kind="ExternalOutput").ap()
    macaron_block(nc, *(dram[name] for name in given), out)
    return run_bass_kernel_spmd(nc, [arrays], core_ids=[0]).results[0]["out"]
```

```python
from contextlib import ExitStack

import numpy as np

import concourse.bass as bass
from concourse import mybir

F32 = mybir.dt.float32
F32R = mybir.dt.float32r
U32 = mybir.dt.uint32
ALU = mybir.AluOpType
ACT = mybir.ActivationFunctionType
AX_X = mybir.AxisListType.X

P = 128
EPS = 1e-5
Q, K, V, O = range(4)
TWO_PI = (6.28125, 0.0019350051879882812, 3.019916050448e-07)
ROUND = 12582912.0


def macaron_block(nc, x_in, w_gate, w_up, w_down, w_router, basis, phase, amp, out):
    _, S, D = x_in.shape
    E = w_router.shape[2]
    CH = w_gate.shape[1]
    HARM = basis.shape[3]
    TILES = S // P
    BLOCKS = 2
    BT = TILES // BLOCKS
    BW = S // BLOCKS
    DH = D // P
    SUB = P // E
    HD = 16
    HEADS = D // HD
    GH = 4
    GROUPS = HEADS // GH
    UNITS = GROUPS * BLOCKS
    KT = TILES
    STEPS = UNITS * KT
    ITEMS = GH * BT
    PER_STEP = ITEMS // KT
    LEAD = 10 * PER_STEP
    WARM_UP = 20
    SCALE = 1.0 / HD ** 0.5
    assert (S, D, HARM, BW, SUB) == (1024, 256, 64, 512, 16)

    def step_stages(s):
        ahead = [("ITEM", it) for it in range(LEAD + PER_STEP * s, LEAD + PER_STEP * (s + 1)) if it < UNITS * ITEMS]
        st = [("SCORES", s, 0), ("SCORES", s, 1)] + ahead[0:1]
        st += [("SCORES", s, 2)]
        st += [("PV", s - 1)] if s > 0 else []
        st += [("PV_OUT", s // KT - 1)] if s % KT == 0 and s > 0 else []
        st += [("MAXIMA", (s + 2) // KT)] if (s + 2) % KT == 0 and s + 2 < STEPS else []
        st += [("SCORES", s, 3)] + ahead[1:2]
        st += [("TURN", s // KT - 1)] if s % KT == 1 and s > KT else []
        st += [("NORMALISE", s // KT - 1)] if s % KT == 2 and s > KT else []
        return st

    stages = [("WARM", WARM_UP), ("SPLIT", "router", 0), ("STATS", 0), ("LN", 0), ("XN", 0), ("SPLIT", "gate", 0),
              ("SPLIT", "up", 0), ("XT", 0), ("ANGLE",), ("ROUTE", 0), ("SINE",), ("TOP", 0), ("GU", 0, 0),
              ("SPLIT", "gate", 1), ("SPLIT", "up", 1), ("STATS", 1), ("LN", 1), ("GU", 0, 1), ("XN", 1),
              ("SPREAD", 0), ("SPLIT", "gate", 2), ("SPLIT", "up", 2), ("GU", 0, 2), ("SPLIT", "down", 0),
              ("GU", 0, 3), ("SPLIT", "down", 1), ("XT", 1), ("GU", 0, 4), ("SPLIT", "down", 2), ("ROUTE", 1),
              ("HOLO",), ("GU", 0, 5), ("TOP", 1), ("GU", 1, 0), ("GU", 1, 1), ("SPREAD", 1),
              ("SPLIT", "basis", 0), ("GU", 1, 2), ("DOWN", 0, 0), ("STATS", 2), ("GU", 1, 3), ("DOWN", 0, 1),
              ("LN", 2), ("SPLIT", "basis", 1), ("GU", 1, 4), ("XN", 2), ("GU", 1, 5), ("XT", 2), ("FLUSH", 1)]
    stages += [("OWN", "projections"), ("RES", K, 0), ("RES", Q, 0), ("SUM", 1, 0, 3), ("SPLIT", "holo", 0),
               ("QK", K, 0, 0), ("QK", Q, 0, 0), ("SUM", 1, 3, 5), ("SPLIT", "holo", 1), ("RES", V, 0),
               ("SUM", 1, 5, CH), ("ADD", 1, 0), ("STATS", 3), ("ADD", 1, 1), ("LN", 3), ("XN", 3),
               ("QK", K, 1, 0), ("V", 0), ("V", 1), ("WARM", 8, 4), ("HALF", 0, 0), ("WARM", 6, 4), ("XT", 3),
               ("HALF", 1, 0), ("RES", K, 1), ("RES", Q, 1), ("QK", K, 0, 1), ("HALF", 2, 0), ("QK", Q, 1, 0),
               ("HALF", 3, 0), ("RES", V, 1), ("HALF", 4, 0), ("QK", Q, 0, 1), ("HALF", 5, 0), ("QK", K, 1, 1),
               ("HALF", 6, 0), ("QK", Q, 1, 1), ("V", 2), ("V", 3), ("ONES",)]
    stages += [("HALF", i, 0) for i in range(7, ITEMS // 2)] + [("OWN", "ring")]
    for i in range(ITEMS // 2):
        stages += [("HALF", i, 1), ("WARM", 2, 4, 3)]
    stages += [("ITEM", ITEMS), ("MAXIMA", 0)]
    for it in range(ITEMS + 1, LEAD):
        stages += [("ITEM", it), ("WARM", 2, 4, 3)]
    fill = {STEPS - 6: [("OWN", "tail"), ("AT", 0)], STEPS - 5: [("RES", O, 0)],
            STEPS - 4: [("Y", 0), ("STATS", 4), ("Y", 1), ("LN", 4), ("XN", 4)], STEPS - 1: [("XT", 4)]}
    for s in range(STEPS):
        stages += step_stages(s) + fill.get(s, [])
    stages += [("PV", STEPS - 1), ("PV_OUT", UNITS - 1), ("ROUTE", 2), ("TURN", UNITS - 1),
               ("NORMALISE", UNITS - 1), ("GU", 2, 0), ("OWN", "second FFN"), ("AT", 1), ("TOP", 2), ("RES", O, 1),
               ("GU", 2, 1), ("SPREAD", 2), ("Y", 2), ("STATS", 5), ("Y", 3), ("LN", 5), ("XN", 5), ("GU", 2, 2),
               ("GU", 2, 3), ("XT", 5), ("GU", 2, 4), ("GU", 2, 5), ("ROUTE", 3), ("TOP", 3), ("GU", 3, 0),
               ("GU", 3, 1), ("SPREAD", 3), ("GU", 3, 2), ("DOWN", 2, 0), ("DOWN", 2, 1), ("GU", 3, 3),
               ("GU", 3, 4), ("GU", 3, 5), ("FLUSH", 3), ("SUM", 3, 0, 4), ("SUM", 3, 4, CH), ("ADD", 3, 0),
               ("ADD", 3, 1)]

    t_no, t_bank, t_turn = {}, [], []
    banks, used = (6, 7), [0] * 8
    for st in stages:
        if st[0] == "OWN":
            banks = {"projections": (0, 1, 2, 3), "ring": (), "tail": (6, 7), "second FFN": (6, 7)}[st[1]]
            begin = len(t_no)
        for part in range(2 if st[0] in ("XT", "AT") else st[0] in ("ROUTE", "TOP", "SPREAD", "RES", "QK", "V", "Y")):
            t_bank.append(banks[(len(t_no) - (0 if banks == (6, 7) else begin)) % len(banks)])
            t_turn.append(used[t_bank[-1]])
            used[t_bank[-1]] += 1
            t_no[st + (part,)] = len(t_no)

    by_pool = [st for st in stages if st in (("RES", V, 1), ("RES", Q, 1), ("QK", Q, 0, 1))
               or (st[0] == "QK" and st[2] == 1)]
    h_no = {use: n for n, use in enumerate(use for use in t_no if use[0] in ("XT", "AT", "RES", "QK")
                                           and use[:-1] not in by_pool)}

    r_no = {st: n for n, st in enumerate(st for st in stages if st[0] in ("SCORES", "MAXIMA", "TURN"))}
    w_no = {st: n for n, st in enumerate(st for st in stages if st[0] == "SPLIT")}

    with ExitStack() as ctx:
        def sb(name, shape, dt=F32):
            return ctx.enter_context(nc.sbuf_tensor(name, shape, dt))

        def sem(name):
            return ctx.enter_context(nc.semaphore(name))

        x = sb("x", [P, TILES, D])
        xn = sb("xn", [P, TILES, D])
        xt_hi = sb("xt_hi", [P, DH, S], F32R)
        xt_lo = sb("xt_lo", [P, DH, S], F32R)
        gate_hi = sb("gate_hi", [P, CH, DH, P], F32R)
        gate_lo = sb("gate_lo", [P, CH, DH, P], F32R)
        up_hi = sb("up_hi", [P, CH, DH, P], F32R)
        up_lo = sb("up_lo", [P, CH, DH, P], F32R)
        down_hi = sb("down_hi", [P, CH, D], F32R)
        down_lo = sb("down_lo", [P, CH, D], F32R)
        router_hi = sb("router_hi", [P, DH, E], F32R)
        router_lo = sb("router_lo", [P, DH, E], F32R)
        basis_hi = sb("basis_hi", [P, 4, DH, P], F32R)
        basis_lo = sb("basis_lo", [P, 4, DH, P], F32R)
        holo_hi = sb("holo_hi", [P, 4, 2, P], F32R)
        holo_lo = sb("holo_lo", [P, 4, 2, P], F32R)
        res = sb("res", [P, 3, S], F32R)
        v_mem = sb("v_mem", [P, KT * HEADS * 32])
        v1 = v_mem[:, :].rearrange("p (k h c) -> p k h c", k=KT, h=HEADS)
        small = 2 * D
        basis_in = v_mem[:, 0:4 * DH * HARM].rearrange("p (w h r) -> p w h r", w=4, h=DH)
        phase_in, amp_in, cos_t, cos_n = (v_mem[:, (i + 1) * small:(i + 2) * small] for i in range(4))
        router_in = sb("router_in", [P, DH, E])
        PIECE = GH * BW
        MAX_ROW = 96
        big = sb("big", [P, 8 * PIECE], F32R)
        hid = big[:, 0:4 * CH * BW].rearrange("p (g a m t) -> p g a m t", g=2, a=2, m=CH)
        piece = [big[:, i * PIECE:(i + 1) * PIECE] for i in range(8)]
        ks, qs = ([[piece[i][0:MAX_ROW + 2, :].rearrange("p (j t) -> p j t", j=GH) for i in two] for two in both]
                  for both in (((2, 3), (6, 7)), ((1, 4), (0, 5))))
        qk_parts = [[piece[i].rearrange("p (a h t) -> p a h t", a=2, h=2) for i in two] for two in ((0, 5), (6, 7))]
        many = sb("many", [P, 3 * CH * D])
        gate_in = many[:, 0:CH * D].rearrange("p (m h f) -> p m h f", m=CH, h=DH)
        up_in = many[:, CH * D:2 * CH * D].rearrange("p (m h f) -> p m h f", m=CH, h=DH)
        down_in = many[:, 2 * CH * D:3 * CH * D].rearrange("p (m d) -> p m d", m=CH)
        holo_in = many[:, 0:4 * D].rearrange("p (w h o) -> p w h o", w=4, h=2)
        probs = many[:, 0:8 * BW].rearrange("p (n t) -> p n t", n=8)
        ident = sb("ident", [P, P])
        zeros = sb("zeros", [P, P])
        expert_no = sb("expert_no", [P, BT, E])
        minus_half = sb("minus_half", [P, BT])
        stats = sb("stats", [P, BT, 6])
        mean_var = sb("mean_var", [P, BT, 2])
        var_eps = sb("var_eps", [P, BT])
        rstd = sb("rstd", [P, BT])
        NH = 5
        feat = sb("feat", [P, NH, BW])
        route_w = sb("route_w", [P, 2, BW])
        score_t = sb("score_t", [E, BW])
        score = sb("score", [P, BT, E])
        top8 = sb("top8", [P, BT, E])
        top_no = sb("top_no", [P, BT, E], U32)
        top_nf = sb("top_nf", [P, BT, 2])
        gap = sb("gap", [P, BT, 1])
        second = sb("second", [P, BT, 1])
        prob = sb("prob", [P, 2, BT, 1])
        chosen = sb("chosen", [P, 2, BT, E])
        spread = sb("spread", [P, BT, E, SUB])
        neg_max = sb("neg_max", [P, 2, ITEMS])
        half_max = sb("half_max", [P, 2, ITEMS])
        max_parts = sb("max_parts", [P, 2 * ITEMS], F32R)
        max_rows = sb("max_rows", [2 * ITEMS, P])
        pv_t = feat[:, 0, :]
        pv_q = feat[:, 1, :].rearrange("p (i j c) -> p i j c", i=BT, j=GH)
        rden = sb("rden", [P, BT, GH])
        bank = [ctx.enter_context(nc.psum_tensor(f"bank{i}", [P, 512], F32)) for i in range(4)]
        pair = [ctx.enter_context(nc.psum_tensor(f"pair{i}", [P, 2, 512], F32)) for i in range(2)]
        banks8 = [b[:, :] for b in bank] + [p[:, c, :] for p in pair for c in range(2)]

        def ffn_banks(g, m):
            return [banks8[b] for b in (((0, 2), (1, 3)) if g < 2 else ((4, 5), (0, 1)))[m % 2]]

        down_b = [banks8[b] for b in (4, 5, 2, 3)]
        sum_b = [[banks8[b] for b in (4, 5, 6, 7)], [banks8[b] for b in (2, 3, 6, 7)]]
        t_b = [banks8[b] for b in t_bank]
        ring_b = banks8[0:3]
        pv_b = banks8[3]
        qk_dram = nc.dram_tensor("qk_parts_dram", (2, 2, D, S), F32).ap()
        x_first_s = sem("x_first_tiles_loaded")
        x_in_s = [sem(f"x_loaded{b}") for b in range(BLOCKS)]
        gate_in_s = [sem(f"gate_loaded{k}") for k in range(3)]
        up_in_s = [sem(f"up_loaded{k}") for k in range(3)]
        down_in_s, router_in_s = sem("down_loaded"), sem("router_loaded")
        phase_in_s, small_in_s, holo_in_s = sem("phase_loaded"), sem("basis_amp_loaded"), sem("holo_copied")
        const_s = sem("constants_ready")
        t_full = sem("t_full")
        t_free = [sem(f"t_free{i}") for i in range(8)]
        w_hi_s, w_lo_s = sem("weight_hi_ready"), sem("weight_lo_ready")
        hi_s = sem("hi_part_ready")
        whole_s = sem("whole_and_hi_ready")
        step_s = sem("vector_step")
        var_s, rstd_s, xn_s = sem("var_ready"), sem("rstd_ready"), sem("xn_ready")
        gate_full, up_full = sem("gate_full"), sem("up_full")
        tanh_s, silu_s = sem("tanh_ready"), sem("silu_ready")
        gated_s, weighed_s = sem("gated_ready"), sem("weighed_ready")
        hid_hi_s, hid_lo_s = sem("hid_hi_ready"), sem("hid_lo_ready")
        down_full, x_s = sem("down_full"), sem("x_updated")
        gap_s, second_s, spread_s = sem("gap_ready"), sem("second_ready"), sem("spread_ready")
        angle_s, sine_s, holo_s = sem("angle_ready"), sem("sine_ready"), sem("holo_ready")
        ones_s = sem("ones_ready")
        zero_rows_s = [sem(f"zero_rows_written{i}") for i in range(2)]
        first_s = [[sem(f"first_{'qk'[w]}_stored{b}") for b in range(BLOCKS)] for w in range(2)]
        rest_s = sem("other_heads_stored")
        k_stack_s = [[sem(f"k_stack_loaded{i}{b}") for b in range(BLOCKS)] for i in range(2)]
        q_stack_s = [[sem(f"q_stack_loaded{i}{b}") for b in range(BLOCKS)] for i in range(2)]
        half_full, half_read = sem("half_items_full"), sem("half_items_read")
        item_full, item_read = sem("item_full"), sem("item_read")
        max_parts_s, max_in_s = sem("max_parts_ready"), sem("max_rows_placed")
        ring_full, ring_read = sem("ring_full"), sem("ring_read")
        pv_s, pv_read = sem("pv_steps_done"), sem("pv_read")
        att_s = sem("attention_unit_ready")
        out_s = sem("out_stored")

        x_tok = x_in.rearrange("a (p i) d -> (a p) i d", p=P)
        out_tok = out.rearrange("a (p i) d -> (a p) i d", p=P)
        def freed(eng, n):
            eng.wait_ge(t_free[t_bank[n]], t_turn[n] + 1)

        def bank_uses(banks_wanted, before):
            first = stages.index(before)
            uses = [t_no[st + (part,)] for st in stages[:first] for part in range(2) if st + (part,) in t_no]
            return [(b, sum(t_bank[n] == b for n in uses)) for b in banks_wanted]

        def lo_ready(eng, name, k):
            eng.wait_ge(w_lo_s, w_no[("SPLIT", name, k)] + 1)

        def block_of(b):
            return slice(b * BW, (b + 1) * BW)

        def tiles_of(b):
            return slice(b * BT, (b + 1) * BT)

        def split_of(st, part):
            if st[0] in ("XT", "AT"):
                b = st[1] % BLOCKS
                return xt_hi[:, part, block_of(b)], xt_lo[:, part, block_of(b)]
            _, w, hf, b = st
            return qk_parts[w][b][:, 0, hf, :], qk_parts[w][b][:, 1, hf, :]

        def pool_part(st):
            if st[0] == "RES":
                return slice(HARM, P), res[:, st[1] % 3, block_of(st[2])], res[HARM:P, st[1] % 3, block_of(st[2])]
            return (slice(0, P), *split_of(st, 0))

        def weights_of(name, k):
            two = slice(2 * k, 2 * k + 2)
            if name == "router":
                return router_in[:, :, :], router_hi[:, :, :], router_lo[:, :, :]
            if name == "basis":
                src = basis_in[:, two, :, :].rearrange("p w h r -> p (w h) r").unsqueeze(2)
                hi, lo = (t[:, two, :, :].rearrange("p w h (c r) -> p (w h) c r", c=2) for t in (basis_hi, basis_lo))
                return src.broadcast_to([P, 2 * DH, 2, HARM]), hi, lo
            if name == "holo":
                return holo_in[:, two, :, :], holo_hi[:, two, :, :], holo_lo[:, two, :, :]
            if name == "down":
                return down_in[:, two, :], down_hi[:, two, :], down_lo[:, two, :]
            src, hi, lo = {"gate": (gate_in, gate_hi, gate_lo), "up": (up_in, up_hi, up_lo)}[name]
            return src[:, two, :, :], hi[:, two, :, :], lo[:, two, :, :]

        def weights_in(eng, name, k):
            if name in ("gate", "up"):
                eng.wait_ge((gate_in_s if name == "gate" else up_in_s)[k], 16)
            elif name == "holo":
                eng.wait_ge(holo_in_s, 16 * 4)
            else:
                eng.wait_ge({"router": router_in_s, "down": down_in_s, "basis": small_in_s}[name],
                            16 * {"router": 1, "down": 1, "basis": 2}[name])

        def seen_as(bank_ap, like):
            dims = list(like.shape)[1:]
            flat = bank_ap[:, 0:int(np.prod(dims))]
            if len(dims) == 1:
                return flat
            if len(dims) == 2:
                return flat.rearrange("p (a b) -> p a b", a=dims[0])
            return flat.rearrange("p (a b c) -> p a b c", a=dims[0], b=dims[1])

        block = ctx.enter_context(nc.Block())

        @block.sync
        def _(sp):
            sp.dma_start(x[:, 0:2, :], x_tok[:, 0:2, :]).then_inc(x_first_s, 16)
            sp.dma_start(x[:, 2:BT, :], x_tok[:, 2:BT, :]).then_inc(x_in_s[0], 16)
            sp.dma_start(router_in[:, :, :], w_router).then_inc(router_in_s, 16)
            for k in range(3):
                two = slice(2 * k, 2 * k + 2)
                sp.dma_start(gate_in[:, two, :, :], w_gate[:, two, :, :]).then_inc(gate_in_s[k], 16)
                sp.dma_start(up_in[:, two, :, :], w_up[:, two, :, :]).then_inc(up_in_s[k], 16)
                if k == 0:
                    sp.dma_start(phase_in, phase.rearrange("p w o -> p (w o)")).then_inc(phase_in_s, 16)
                    sp.dma_start(x[:, BT:TILES, :], x_tok[:, BT:TILES, :]).then_inc(x_in_s[1], 16)
            sp.dma_start(down_in, w_down).then_inc(down_in_s, 16)
            sp.dma_start(basis_in, basis).then_inc(small_in_s, 16)
            sp.dma_start(amp_in, amp.rearrange("p w o -> p (w o)")).then_inc(small_in_s, 16)
            sp.wait_ge(holo_s, 1)
            lo_ready(sp, "gate", 2)
            for pr in range(2):
                for c in range(2):
                    sp.dma_start(holo_in[c * HARM:(c + 1) * HARM, 2 * pr:2 * pr + 2, :, :],
                                 cos_t[pr * HARM:(pr + 1) * HARM, :].rearrange("p (w h o) -> p w h o", w=2, h=2)
                                 ).then_inc(holo_in_s, 16)

            def store(w, b, hf, rows, signal):
                freed(sp, t_no[("QK", w, hf, b, 0)])
                sp.dma_start(qk_dram[w][:, hf * P + rows.start:hf * P + rows.stop, block_of(b)]
                             .rearrange("a p t -> p a t"),
                             qk_parts[w][b][rows, :, hf, :].bitcast(F32)).then_inc(signal, 16)

            def load(w, b, hg):
                dst = (qs if w == Q else ks)[hg % 2][b]
                for c, part in enumerate((0, 1, 0, 1) if w == Q else (0, 0, 1, 1)):
                    sp.dma_start(dst[c * HD:(c + 1) * HD, :, :].bitcast(F32),
                                 qk_dram[w][part, hg * GH * HD:(hg + 1) * GH * HD, block_of(b)]
                                 .rearrange("(j d) t -> d j t", j=GH)
                                 ).then_inc((q_stack_s if w == Q else k_stack_s)[hg % 2][b], 16)

            def zero_rows(i):
                for dst in ks[i] + qs[i]:
                    sp.dma_start(dst[64:MAX_ROW, :, :].bitcast(F32).rearrange("p j (a c) -> p (j a) c", c=P),
                                 zeros[64:MAX_ROW, :].unsqueeze(1).broadcast_to([MAX_ROW - 64, PIECE // P, P])
                                 ).then_inc(zero_rows_s[i], 16)

            def load_stacks(hg):
                if hg == 1:
                    sp.wait_ge(rest_s, 16 * 8)
                    zero_rows(1)
                else:
                    sp.wait_ge(pv_s, 2 * KT * (hg - 1))
                for b in range(BLOCKS):
                    load(K, b, hg)
                for b in range(BLOCKS):
                    load(Q, b, hg)

            first, others = slice(0, GH * HD), slice(GH * HD, P)
            for w in (K, Q):
                store(w, 0, 0, first, first_s[w][0])
            sp.wait_ge(x_s, 2)
            for w in (K, Q):
                sp.wait_ge(first_s[w][0], 16)
                load(w, 0, 0)
            sp.wait_ge(x_s, 4)
            zero_rows(0)
            for w in (K, Q):
                store(w, 1, 0, first, first_s[w][1])
                sp.wait_ge(first_s[w][1], 16)
                load(w, 1, 0)
            for b in range(BLOCKS):
                for w in (K, Q):
                    store(w, b, 0, others, rest_s)
                    store(w, b, 1, slice(0, P), rest_s)
            for u in range(UNITS):
                hg, b = u // BLOCKS, u % BLOCKS
                sp.wait_ge(ring_read, r_no[("MAXIMA", u)] + 1)
                for part in range(2):
                    sp.dma_start(qs[hg % 2][b][MAX_ROW + part:MAX_ROW + part + 1, :, :].bitcast(F32)
                                 .rearrange("o j (i c) -> o (j i) c", c=P),
                                 max_rows[part * ITEMS:(part + 1) * ITEMS, :]).then_inc(max_in_s, 16)
                if u in (0, 2, 4):
                    load_stacks(u // 2 + 1)
            for i in range(TILES // 2):
                two = slice(2 * i, 2 * i + 2)
                sp.wait_ge(x_s, 2 * BLOCKS + i + 1)
                sp.dma_start(out_tok[:, two, :], x[:, two, :]).then_inc(out_s, 16)
            sp.wait_ge(out_s, 16 * (TILES // 2))

        @block.gpsimd
        def _(pool):
            pool.memset(zeros[:, :], 0.0).then_inc(const_s, 1)
            pool.wait_ge(const_s, 1)
            pool.affine_select(out=ident[:, :], in_=zeros[:, :], compare_op=ALU.not_equal, fill=1.0, base=0,
                               pattern=[[-1, P]], channel_multiplier=1).then_inc(const_s, 1)
            pool.memset(minus_half[:, :], -0.5).then_inc(const_s, 1)
            for e in range(E):
                pool.memset(expert_no[:, :, e:e + 1], float(e)).then_inc(const_s, 1)

            def split_lo(st):
                src, hi, lo = weights_of(*st[1:])
                pool.wait_ge(w_hi_s, w_no[st] + 1)
                pool.tensor_tensor(lo, src, hi.bitcast(F32), ALU.subtract).then_inc(w_lo_s, 1)

            def weigh(n):
                g, m = n // CH, n % CH
                pool.wait_ge(gated_s, n + 1)
                if m == 0:
                    freed(pool, t_no[("SPREAD", g, 0)])
                pool.tensor_tensor(feat[:, n % NH, :], feat[:, n % NH, :], route_w[:, g % 2, :],
                                   ALU.mult).then_inc(weighed_s, 1)

            for st in stages:
                if st[0] == "LN":
                    l = st[1]
                    pool.wait_ge(var_s, l + 1)
                    if l == 0:
                        pool.wait_ge(const_s, 3)
                    else:
                        pool.wait_ge(xn_s, l)
                    pool.tensor_tensor(rstd[:, :], var_eps[:, :], minus_half[:, :], ALU.pow).then_inc(rstd_s, 1)
                elif st[0] == "SPLIT":
                    split_lo(st)
                elif st[0] == "GU":
                    n = st[1] * CH + st[2]
                    if n % (2 * CH):
                        weigh(n - 1)
                elif st[0] == "FLUSH":
                    weigh((st[1] + 1) * CH - 1)
                elif st in by_pool:
                    i, n = by_pool.index(st), t_no[st + (0,)]
                    rows, hi, lo = pool_part(st)
                    pool.wait_ge(whole_s, i + 1)
                    if i >= 1:
                        freed(pool, t_no[by_pool[i - 1] + (0,)])
                    pool.tensor_tensor(lo, feat[rows, 2 + i % 3, :], hi[rows, :].bitcast(F32), ALU.subtract
                                       ).then_inc(t_free[t_bank[n]], 1)
                elif st[0] == "ONES":
                    freed(pool, t_no[by_pool[-1] + (0,)])
                    lo_ready(pool, "basis", 1)
                    pool.wait_ge(holo_in_s, 16 * 4)
                    pool.memset(v1[:, :, :, HD:32], 1.0).then_inc(ones_s, 1)
                    pool.wait_ge(x_s, 4)
                    pool.wait_ge(rstd_s, 4)
                    for b in range(BLOCKS):
                        pool.wait_ge(ones_s, 1 + b)
                        pool.memset(ks[0][b][MAX_ROW:MAX_ROW + 2, :, :].bitcast(F32), 1.0).then_inc(ones_s, 1)
                elif st == ("OWN", "ring"):
                    pool.wait_ge(rest_s, 16 * 8)
                    for w in (Q, K):
                        for b in range(BLOCKS):
                            pool.wait_ge(first_s[w][b], 16)
                    for b in range(BLOCKS):
                        pool.wait_ge(ones_s, 3 + b)
                        pool.memset(ks[1][b][MAX_ROW:MAX_ROW + 2, :, :].bitcast(F32), 1.0).then_inc(ones_s, 1)

        @block.scalar
        def _(act):
            def hid_hi(n):
                g, m = n // CH, n % CH
                act.wait_ge(weighed_s, n + 1)
                act.copy(hid[:, g % 2, 0, m, :], feat[:, n % NH, :]).then_inc(hid_hi_s, 1)

            for st in stages:
                kind = st[0]
                if kind == "SPLIT":
                    src, hi, _ = weights_of(*st[1:])
                    weights_in(act, *st[1:])
                    act.copy(hi, src).then_inc(w_hi_s, 1)
                elif st in by_pool:
                    i, n = by_pool.index(st), t_no[st + (0,)]
                    rows, hi, _ = pool_part(st)
                    act.wait_ge(t_full, n + 1)
                    act.wait_ge(hid_lo_s, 2 * CH)
                    if i >= 3:
                        freed(act, t_no[by_pool[i - 3] + (0,)])
                    act.copy(feat[rows, 2 + i % 3, :], t_b[n][rows, :])
                    act.copy(hi, t_b[n]).then_inc(whole_s, 1)
                elif kind in ("XT", "AT", "QK"):
                    for part in range(2 if kind in ("XT", "AT") else 1):
                        n = t_no[st + (part,)]
                        hi, _ = split_of(st, part)
                        act.wait_ge(t_full, n + 1)
                        act.copy(hi, seen_as(t_b[n], hi)).then_inc(hi_s, 1)
                elif kind == "RES":
                    _, w, b = st
                    n = t_no[st + (0,)]
                    act.wait_ge(t_full, n + 1)
                    act.copy(res[:, w % 3, block_of(b)], t_b[n]).then_inc(hi_s, 1)
                elif kind == "ROUTE":
                    n = t_no[st + (0,)]
                    act.wait_ge(t_full, n + 1)
                    act.copy(score_t[:, :], t_b[n][0:E, :]).then_inc(t_free[t_bank[n]], 1)
                elif kind == "TOP":
                    act.wait_ge(gap_s, st[1] + 1)
                    act.activation(second[:, :, :], gap[:, :, :], ACT.Exp).then_inc(second_s, 1)
                elif kind == "SPREAD":
                    n = t_no[st + (0,)]
                    if st[1] >= 2:
                        act.wait_ge(weighed_s, CH * (st[1] - 1))
                    act.wait_ge(t_full, n + 1)
                    act.copy(route_w[:, st[1] % 2, :], t_b[n]).then_inc(t_free[t_bank[n]], 1)
                elif kind == "GU":
                    _, g, m = st
                    n = g * CH + m
                    act.wait_ge(gate_full, n + 1)
                    if n >= NH:
                        act.wait_ge(hid_lo_s, n - NH + 1)
                    act.activation(feat[:, n % NH, :], ffn_banks(g, m)[0], ACT.Tanh, scale=0.5).then_inc(tanh_s, 1)
                    if n > n // (2 * CH) * 2 * CH + 1:
                        hid_hi(n - 2)
                elif kind == "FLUSH":
                    hid_hi((st[1] + 1) * CH - 2)
                    hid_hi((st[1] + 1) * CH - 1)
                elif kind == "SINE":
                    act.wait_ge(angle_s, 1)
                    act.activation(cos_n, cos_t, ACT.Sin, scale=0.5).then_inc(sine_s, 1)
                elif kind == "V":
                    n = t_no[st + (0,)]
                    act.wait_ge(t_full, n + 1)
                    act.copy(v1[:, 2 * st[1]:2 * st[1] + 2, :, 0:HD],
                             t_b[n].rearrange("p (i h c) -> p i h c", i=2, h=HEADS)).then_inc(t_free[t_bank[n]], 1)
                elif kind == "MAXIMA":
                    act.wait_ge(ring_full, r_no[st] + 1)
                    if st[1] >= 1:
                        act.wait_ge(max_in_s, 32 * st[1])
                    act.copy(max_rows[:, :], ring_b[r_no[st] % 3][0:2 * ITEMS, 0:P]).then_inc(ring_read, 1)
                elif kind == "SCORES":
                    _, s, j = st
                    act.wait_ge(ring_full, r_no[st] + 1)
                    if s >= 2:
                        act.wait_ge(pv_s, s - 1)
                    act.activation(probs[:, (GH * s + j) % 8, :], ring_b[r_no[st] % 3], ACT.Exp,
                                   scale=SCALE).then_inc(ring_read, 1)
                elif kind == "PV_OUT":
                    act.wait_ge(pv_s, KT * (st[1] + 1))
                    act.copy(pv_t, pv_b).then_inc(pv_read, 1)
                elif kind == "TURN":
                    act.wait_ge(ring_full, r_no[st] + 1)
                    if st[1] >= 1:
                        act.wait_ge(att_s, st[1])
                    act.copy(pv_q, ring_b[r_no[st] % 3].rearrange("p (i j c) -> p i j c", i=BT, j=GH)
                             ).then_inc(ring_read, 1)

        @block.vector
        def _(dve):
            steps = [0]

            def link(ins):
                steps[0] += 1
                ins.then_inc(step_s, 1)
                dve.wait_ge(step_s, steps[0])

            hi_no = [0]

            def lo_part(n, lo, hi, src):
                hi_no[0] += 1
                dve.wait_ge(hi_s, hi_no[0])
                dve.tensor_tensor(lo, src, hi.bitcast(F32), ALU.subtract).then_inc(t_free[t_bank[n]], 1)

            def half_stats(l, half):
                b = l % BLOCKS
                if l < 2:
                    dve.wait_ge(x_first_s if (l, half) == (0, 0) else x_in_s[b], 16)
                elif l < 4:
                    dve.wait_ge(x_s, 2 * b + half + 1)
                else:
                    freed(dve, t_no[("Y", 2 * b + half, 0)])
                for i in (2 * half, 2 * half + 1):
                    ins = dve.bn_stats(stats[:, i, :], x[:, b * BT + i, :])
                return ins

            def variance(l):
                link(half_stats(l, 1))
                for i in range(BT):
                    ins = dve.bn_aggr(mean_var[:, i, :], stats[:, i, :])
                link(ins)
                dve.tensor_scalar(var_eps[:, :], mean_var[:, :, 1], EPS, None, ALU.add).then_inc(var_s, 1)

            def normal_x(l):
                b = l % BLOCKS
                dve.wait_ge(rstd_s, l + 1)
                for i in range(BT):
                    ins = dve.tensor_scalar(xn[:, b * BT + i, :], x[:, b * BT + i, :], mean_var[:, i, 0:1],
                                            rstd[:, i:i + 1], ALU.subtract, ALU.mult)
                ins.then_inc(xn_s, 1)

            def route(g, n):
                dve.wait_ge(t_full, n + 1)
                if g == 0:
                    dve.wait_ge(const_s, 3 + E)
                ins = dve.tensor_copy(score[:, :, :], t_b[n][:, 0:BT * E].rearrange("p (i e) -> p i e", i=BT))
                ins.then_inc(t_free[t_bank[n]], 1)
                freed(dve, n)
                for i in range(BT):
                    ins = dve.max(top8[:, i, :], score[:, i, :])
                link(ins)
                for i in range(BT):
                    ins = dve.max_index(top_no[:, i, :], top8[:, i, :], score[:, i, :])
                link(ins)
                dve.tensor_tensor(gap[:, :, :], top8[:, :, 1:2], top8[:, :, 0:1], ALU.subtract).then_inc(gap_s, 1)
                link(dve.tensor_copy(top_nf[:, :, :], top_no[:, :, 0:2]))
                for c in range(2):
                    ins = dve.tensor_tensor(chosen[:, c, :, :], expert_no[:, :, :],
                                            top_nf[:, :, c:c + 1].broadcast_to([P, BT, E]), ALU.is_equal)
                link(ins)
                dve.wait_ge(second_s, g + 1)
                link(dve.tensor_scalar(prob[:, 1, :, :], second[:, :, :], 4.0, 4.0, ALU.mult, ALU.add))
                link(dve.reciprocal(prob[:, 0, :, :], prob[:, 1, :, :]))
                link(dve.tensor_tensor(prob[:, 1, :, :], prob[:, 0, :, :], second[:, :, :], ALU.mult))
                for c in range(2):
                    ins = dve.tensor_tensor(chosen[:, c, :, :], chosen[:, c, :, :],
                                            prob[:, c, :, :].broadcast_to([P, BT, E]), ALU.mult)
                link(ins)
                link(dve.tensor_tensor(chosen[:, 0, :, :], chosen[:, 0, :, :], chosen[:, 1, :, :], ALU.add))
                dve.tensor_copy(spread[:, :, :, :].rearrange("p i e r -> p (i e) r"),
                                chosen[:, 0, :, :].rearrange("p i e -> p (i e)").unsqueeze(2)
                                .broadcast_to([P, BT * E, SUB])).then_inc(spread_s, 1)

            def normalise(u):
                hg, b = u // BLOCKS, u % BLOCKS
                dve.wait_ge(ring_read, r_no[("TURN", u)] + 1)
                link(dve.reciprocal(rden[:, :, :], pv_q[:, :, :, HD]))
                dve.tensor_tensor(xn[:, tiles_of(b), hg * GH * HD:(hg + 1) * GH * HD]
                                  .rearrange("p i (j c) -> p i j c", j=GH),
                                  pv_q[:, :, :, 0:HD],
                                  rden[:, :, :].unsqueeze(3).broadcast_to([P, BT, GH, HD]), ALU.mult).then_inc(att_s, 1)

            def parts_of_maxima(u):
                if u >= 1:
                    dve.wait_ge(ring_full, r_no[("MAXIMA", u - 1)] + 1)
                link(dve.tensor_copy(max_parts[:, 0:ITEMS], neg_max[:, u % 2, :]))
                dve.tensor_tensor(max_parts[:, ITEMS:2 * ITEMS], neg_max[:, u % 2, :],
                                  max_parts[:, 0:ITEMS].bitcast(F32), ALU.subtract).then_inc(max_parts_s, 1)

            def hid_lo(n):
                g, m = n // CH, n % CH
                dve.wait_ge(hid_hi_s, n + 1)
                dve.tensor_tensor(hid[:, g % 2, 1, m, :], feat[:, n % NH, :],
                                  hid[:, g % 2, 0, m, :].bitcast(F32), ALU.subtract).then_inc(hid_lo_s, 1)

            for st in stages:
                kind = st[0]
                if kind == "STATS":
                    half_stats(st[1], 0)
                elif kind == "LN":
                    variance(st[1])
                elif kind == "XN":
                    normal_x(st[1])
                elif st in by_pool:
                    pass
                elif kind in ("XT", "AT", "QK"):
                    for part in range(2 if kind in ("XT", "AT") else 1):
                        n = t_no[st + (part,)]
                        hi, lo = split_of(st, part)
                        lo_part(n, lo, hi, seen_as(t_b[n], hi))
                elif kind == "RES":
                    _, w, b = st
                    n = t_no[st + (0,)]
                    both = res[HARM:2 * HARM, w % 3, block_of(b)]
                    lo_part(n, both, both, t_b[n][HARM:2 * HARM, :])
                elif kind == "TOP":
                    route(st[1], t_no[st + (0,)])
                elif kind == "GU":
                    _, g, m = st
                    n = g * CH + m
                    dve.wait_ge(tanh_s, n + 1)
                    dve.scalar_tensor_tensor(out=feat[:, n % NH, :], in0=feat[:, n % NH, :], scalar=1.0,
                                             in1=ffn_banks(g, m)[0], op0=ALU.add, op1=ALU.mult).then_inc(silu_s, 1)
                    dve.wait_ge(silu_s, n + 1)
                    dve.wait_ge(up_full, n + 1)
                    dve.tensor_tensor(feat[:, n % NH, :], feat[:, n % NH, :], ffn_banks(g, m)[1],
                                      ALU.mult).then_inc(gated_s, 1)
                    if n > n // (2 * CH) * 2 * CH + 1:
                        hid_lo(n - 2)
                elif kind == "FLUSH":
                    hid_lo((st[1] + 1) * CH - 2)
                    hid_lo((st[1] + 1) * CH - 1)
                elif kind == "DOWN":
                    _, g, i = st
                    dve.wait_ge(down_full, 2 * g + i + 1)
                    tiles = slice(g % 2 * BT + 2 * i, g % 2 * BT + 2 * i + 2)
                    dve.tensor_tensor(x[:, tiles, :], x[:, tiles, :],
                                      down_b[g // 2 * 2 + i].rearrange("p (a d) -> p a d", a=2),
                                      ALU.add).then_inc(x_s, 1)
                elif kind == "ADD":
                    _, g, i = st
                    dve.wait_ge(down_full, 2 * g + i + 1)
                    for t in (2 * i, 2 * i + 1):
                        ins = dve.tensor_tensor(x[:, BT + t, :], x[:, BT + t, :], sum_b[g // 2][t][:, 0:D], ALU.add)
                    ins.then_inc(x_s, 1)
                elif kind == "Y":
                    n = t_no[st + (0,)]
                    tiles = slice(2 * st[1], 2 * st[1] + 2)
                    dve.wait_ge(t_full, n + 1)
                    dve.tensor_tensor(x[:, tiles, :], x[:, tiles, :],
                                      t_b[n].rearrange("p (a d) -> p a d", a=2), ALU.add).then_inc(t_free[t_bank[n]], 1)
                elif kind == "ANGLE":
                    ph = phase_in
                    dve.wait_ge(phase_in_s, 16)
                    link(dve.tensor_scalar(cos_n, ph, 1.0 / (2.0 * np.pi), ROUND, ALU.mult, ALU.add))
                    link(dve.tensor_scalar(cos_n, cos_n, ROUND, None, ALU.subtract))
                    link(dve.scalar_tensor_tensor(out=cos_t, in0=cos_n, scalar=-TWO_PI[0], in1=ph,
                                                  op0=ALU.mult, op1=ALU.add))
                    link(dve.scalar_tensor_tensor(out=cos_t, in0=cos_n, scalar=-TWO_PI[1], in1=cos_t,
                                                  op0=ALU.mult, op1=ALU.add))
                    dve.scalar_tensor_tensor(out=cos_t, in0=cos_n, scalar=-TWO_PI[2], in1=cos_t,
                                             op0=ALU.mult, op1=ALU.add).then_inc(angle_s, 1)
                elif kind == "HOLO":
                    dve.wait_ge(sine_s, 1)
                    dve.wait_ge(small_in_s, 16 * 2)
                    link(dve.tensor_tensor(cos_t, cos_n, cos_n, ALU.mult))
                    link(dve.tensor_scalar(cos_n, cos_t, -2.0, 1.0, ALU.mult, ALU.add))
                    dve.tensor_tensor(cos_t, cos_n, amp_in, ALU.mult).then_inc(holo_s, 1)
                elif kind == "ITEM":
                    u, i = st[1] // ITEMS, st[1] % ITEMS
                    dve.wait_ge(item_full, st[1] + 1 - ITEMS)
                    dve.tensor_reduce(neg_max[:, u % 2, i:i + 1],
                                      pair[st[1] % 2][:, :, :].rearrange("p a b -> p (a b)"),
                                      AX_X, ALU.max, negate=True).then_inc(item_read, 1)
                    if i == ITEMS - 1:
                        dve.wait_ge(item_read, st[1] + 1 - ITEMS)
                        parts_of_maxima(u)
                elif kind == "HALF":
                    _, i, c = st
                    n = c * ITEMS // 2 + i
                    dve.wait_ge(half_full, n + 1)
                    dve.tensor_reduce(half_max[:, c, 2 * i:2 * i + 2], pair[n % 2][:, :, :], AX_X, ALU.max,
                                      negate=True).then_inc(half_read, 1)
                    if n == ITEMS - 1:
                        dve.wait_ge(half_read, n + 1)
                        link(dve.tensor_tensor(neg_max[:, 0, :], half_max[:, 0, :], half_max[:, 1, :], ALU.min))
                        parts_of_maxima(0)
                elif kind == "NORMALISE":
                    normalise(st[1])

        @block.tensor
        def _(pe):
            PASSES = ((0, 0), (0, 1), (1, 0))

            def take(n):
                if t_turn[n] > 0:
                    pe.wait_ge(t_free[t_bank[n]], t_turn[n])
                elif t_bank[n] < 4:
                    pe.wait_ge(silu_s if t_bank[n] < 2 else gated_s, 2 * CH - 1 + t_bank[n] % 2)
                return t_b[n]

            def product(dst, stationary, moving, source=None):
                for c, (a, b, dh) in enumerate((a, b, dh) for a, b in ((0, 0), (1, 0), (0, 1)) for dh in range(DH)):
                    if source and c < DH:
                        pe.wait_ge(hi_s, h_no[source + (dh,)] + 1)
                    elif source and b:
                        freed(pe, t_no[source + (dh,)])
                    ins = pe.matmul(dst, stationary[a](dh), moving[b](dh), start=(c == 0), stop=(c == 3 * DH - 1))
                return ins

            def xt(b):
                return [lambda dh: xt_hi[:, dh, block_of(b)], lambda dh: xt_lo[:, dh, block_of(b)]]

            def turned(n, sources, width=P, rows=P):
                dst = take(n)
                for c, src in enumerate(sources):
                    ins = pe.transpose(dst[:, c * width:(c + 1) * width], src, ident[0:rows, 0:rows])
                ins.then_inc(t_full, 1)

            def item(it):
                u, i = it // ITEMS, it % ITEMS
                hg, b = u // BLOCKS, u % BLOCKS
                j, tile = i // BT, i % BT
                if b == 0 and i == 0:
                    for c in range(BLOCKS):
                        pe.wait_ge(k_stack_s[hg % 2][c], 4 * 16 * (hg // 2 + 1))
                    pe.wait_ge(zero_rows_s[hg % 2], 4 * 16)
                if i == 0:
                    pe.wait_ge(q_stack_s[hg % 2][b], 4 * 16 * (hg // 2 + 1))
                if it < ITEMS + 2:
                    pe.wait_ge(half_read, it - 1)
                else:
                    pe.wait_ge(item_read, it - 1 - ITEMS)
                for c in range(2):
                    ins = pe.matmul(pair[it % 2][:, c, :], qs[hg % 2][b][0:MAX_ROW, j, tile * P:(tile + 1) * P],
                                    ks[hg % 2][c][0:MAX_ROW, j, :], start=True, stop=True)
                ins.then_inc(item_full, 1)

            def half_items(i, c):
                n = c * ITEMS // 2 + i
                if i == 0:
                    pe.wait_ge(k_stack_s[0][c], 4 * 16)
                if n == 0:
                    pe.wait_ge(q_stack_s[0][0], 4 * 16)
                    pe.wait_ge(x_s, 4)
                if n >= 2:
                    pe.wait_ge(half_read, n - 1)
                rows = MAX_ROW if n >= 2 else 4 * HD
                if n == 2:
                    pe.wait_ge(zero_rows_s[0], 4 * 16)
                for part in range(2):
                    j, tile = (2 * i + part) // BT, (2 * i + part) % BT
                    ins = pe.matmul(pair[n % 2][:, part, :], qs[0][0][0:rows, j, tile * P:(tile + 1) * P],
                                    ks[0][c][0:rows, j, :], start=True, stop=True)
                ins.then_inc(half_full, 1)

            def ring_take(use):
                n = r_no[use]
                if n >= 3:
                    pe.wait_ge(ring_read, n - 2)
                return ring_b[n % 3]

            def maxima(u):
                pe.wait_ge(max_parts_s, u + 1)
                dst = ring_take(("MAXIMA", u))
                pe.transpose(dst[0:2 * ITEMS, 0:P], max_parts[:, :].bitcast(F32), ident[:, :]).then_inc(ring_full, 1)

            def scores(s, j):
                u, kt = s // KT, s % KT
                hg, b = u // BLOCKS, u % BLOCKS
                if kt == 0 and j == 0:
                    pe.wait_ge(max_in_s, 32 * (u + 1))
                    pe.wait_ge(ones_s, 3 if hg == 0 else 5)
                    pe.wait_ge(zero_rows_s[hg % 2], 4 * 16)
                dst = ring_take(("SCORES", s, j))
                pe.matmul(dst[:, :], ks[hg % 2][kt // BT][:, j, kt % BT * P:(kt % BT + 1) * P], qs[hg % 2][b][:, j, :],
                          start=True, stop=True).then_inc(ring_full, 1)

            def weigh_values(s):
                u, kt = s // KT, s % KT
                if s == 0:
                    for i in (TILES // 2 - 2, TILES // 2 - 1):
                        freed(pe, t_no[("V", i, 0)])
                    pe.wait_ge(ones_s, 1)
                if kt == 0 and u >= 1:
                    pe.wait_ge(pv_read, u)
                pe.wait_ge(ring_read, r_no[("SCORES", s, GH - 1)] + 1)
                for j in range(GH):
                    ins = pe.matmul(pv_b[32 * j:32 * j + 32, :], v1[:, kt, u // BLOCKS * GH + j, :],
                                    probs[:, (GH * s + j) % 8, :], start=(kt == 0), stop=(kt == KT - 1))
                ins.then_inc(pv_s, 1)

            def turn(u):
                pe.wait_ge(pv_read, u + 1)
                dst = ring_take(("TURN", u))
                for i in range(BT):
                    ins = pe.transpose(dst[:, i * P:(i + 1) * P], pv_t[:, i * P:(i + 1) * P], ident[:, :])
                ins.then_inc(ring_full, 1)

            def own(phase):
                of = {"projections": (), "ring": (0, 1, 2, 3), "tail": (), "second FFN": ()}[phase]
                for b, uses in bank_uses(of, ("OWN", phase)):
                    if uses:
                        pe.wait_ge(t_free[b], uses)
                if phase == "tail":
                    pe.wait_ge(item_read, (UNITS - 1) * ITEMS)
                elif phase == "second FFN":
                    pe.wait_ge(ring_read, len(r_no))
                    pe.wait_ge(pv_read, UNITS)

            def keep_warm(count, b=7):
                for n in range(count):
                    pe.matmul(banks8[b][:, 0:P], ident[:, :], ident[:, :], start=True, stop=True)

            pe.wait_ge(const_s, 2)
            for st in stages:
                kind = st[0]
                n = t_no.get(st + (0,))
                if kind in ("XT", "AT"):
                    if kind == "XT":
                        pe.wait_ge(xn_s, st[1] + 1)
                    else:
                        pe.wait_ge(att_s, UNITS - 1 + st[1])
                    for dh in range(DH):
                        turned(n + dh, [xn[:, st[1] % BLOCKS * BT + i, dh * P:(dh + 1) * P] for i in range(BT)])
                elif kind == "ROUTE":
                    g = st[1]
                    l = g if g < 2 else g + 2
                    lo_ready(pe, "router", 0)
                    dst = take(n)
                    product(dst[0:E, :], [lambda dh: router_hi[:, dh, :], lambda dh: router_lo[:, dh, :]],
                            xt(g % 2), ("XT", l)).then_inc(t_full, 1)
                elif kind == "TOP":
                    freed(pe, t_no[("ROUTE", st[1], 0)])
                    turned(n, [score_t[:, i * P:(i + 1) * P] for i in range(BT)], E, E)
                elif kind == "SPREAD":
                    pe.wait_ge(spread_s, st[1] + 1)
                    turned(n, [spread[:, i, :, :].rearrange("p e r -> p (e r)") for i in range(BT)])
                elif kind == "GU":
                    _, g, m = st
                    q = g * CH + m
                    if g == 0:
                        lo_ready(pe, "gate", m // 2)
                        lo_ready(pe, "up", m // 2)
                    if q >= 2:
                        pe.wait_ge(silu_s, q - 1)
                    product(ffn_banks(g, m)[0], [lambda dh: gate_hi[:, m, dh, :], lambda dh: gate_lo[:, m, dh, :]],
                            xt(g % 2)).then_inc(gate_full, 1)
                    if q >= 2:
                        pe.wait_ge(gated_s, q - 1)
                    product(ffn_banks(g, m)[1], [lambda dh: up_hi[:, m, dh, :], lambda dh: up_lo[:, m, dh, :]],
                            xt(g % 2)).then_inc(up_full, 1)
                elif kind == "DOWN":
                    _, g, i = st
                    if g == 0:
                        lo_ready(pe, "down", 2)
                    else:
                        pe.wait_ge(x_s, 2 * (g - 1) + i + 1)
                    for c in range(2):
                        at = (2 * i + c) * P
                        for m in range(CH):
                            if i == 0 and c == 0:
                                pe.wait_ge(hid_lo_s, CH * g + m + 1)
                            for k, (a, b) in enumerate(PASSES):
                                ins = pe.matmul(down_b[g // 2 * 2 + i][:, c * D:(c + 1) * D],
                                                hid[:, g % 2, a, m, at:at + P], (down_hi, down_lo)[b][:, m, :],
                                                start=(m == 0 and k == 0),
                                                stop=(m == CH - 1 and k == 2))
                    ins.then_inc(down_full, 1)
                elif kind == "SUM":
                    _, g, begin, end = st
                    order = [(m, t) for m in range(begin, end) for t in range(BT)]
                    if begin == 0:
                        order.sort(key=lambda at: at[1] // 2)
                        pe.wait_ge(x_s, 2 * g)
                    for m, t in order:
                        if (m, t) == (0, 2):
                            for b, uses in bank_uses((6, 7), st):
                                pe.wait_ge(t_free[b], uses)
                        if t == 0:
                            pe.wait_ge(hid_lo_s, CH * g + m + 1)
                        for k, (a, b) in enumerate(PASSES):
                            ins = pe.matmul(sum_b[g // 2][t][:, 0:D], hid[:, g % 2, a, m, t * P:(t + 1) * P],
                                            (down_hi, down_lo)[b][:, m, :], start=(m == 0 and k == 0),
                                            stop=(m == CH - 1 and k == 2))
                        if m == CH - 1 and t % 2:
                            ins.then_inc(down_full, 1)
                elif kind == "RES":
                    _, w, b = st
                    lo_ready(pe, "basis", w // 2)
                    dst = take(n)
                    product(dst, [lambda dh: basis_hi[:, w, dh, :], lambda dh: basis_lo[:, w, dh, :]],
                            xt(b), ("AT", b) if w == O else ("XT", 2 + b)).then_inc(t_full, 1)
                elif kind == "QK":
                    _, w, hf, b = st
                    freed(pe, t_no[("RES", w, b, 0)])
                    lo_ready(pe, "holo", 0)
                    dst = take(n)
                    for c, part in enumerate((holo_hi, holo_lo)):
                        ins = pe.matmul(dst, part[:, w, hf, :], res[:, w % 3, block_of(b)],
                                        start=(c == 0), stop=(c == 1))
                    ins.then_inc(t_full, 1)
                elif kind in ("V", "Y"):
                    w = V if kind == "V" else O
                    freed(pe, t_no[("RES", w, 2 * st[1] // BT, 0)])
                    lo_ready(pe, "holo", 1)
                    dst = take(n)
                    for c in range(2):
                        at = (2 * st[1] + c) * P
                        for k, part in enumerate((holo_hi, holo_lo)):
                            ins = pe.matmul(dst[:, c * D:(c + 1) * D], res[:, w % 3, at:at + P],
                                            part[:, w, :, :].rearrange("p h o -> p (h o)"),
                                            start=(k == 0), stop=(k == 1))
                    ins.then_inc(t_full, 1)
                elif kind == "ITEM":
                    item(st[1])
                elif kind == "HALF":
                    half_items(*st[1:])
                elif kind == "WARM":
                    if len(st) > 2:
                        pe.wait_ge(x_s, st[2])
                    keep_warm(st[1], *st[3:])
                elif kind == "MAXIMA":
                    maxima(st[1])
                elif kind == "SCORES":
                    scores(*st[1:])
                elif kind == "PV":
                    weigh_values(st[1])
                elif kind == "TURN":
                    turn(st[1])
                elif kind == "OWN":
                    own(st[1])


def kernel(L0_attn_hidden_states, L0_attn_basis_q, L0_attn_phase_q, L0_attn_amp_q, L0_attn_basis_k, L0_attn_phase_k,
           L0_attn_amp_k, L0_attn_basis_v, L0_attn_phase_v, L0_attn_amp_v, L0_attn_basis_o, L0_attn_phase_o,
           L0_attn_amp_o, L0_ffn_w_gate_router, L0_ffn_w_gate_proj, L0_ffn_w_up_proj, L0_ffn_w_down_proj):
    import concourse.bacc as bacc
    from concourse.bass_utils import run_bass_kernel_spmd

    w_gate, w_up = (w.reshape(128, 6, 2, 128).transpose(3, 1, 2, 0) for w in (L0_ffn_w_gate_proj, L0_ffn_w_up_proj))
    basis = np.stack([L0_attn_basis_q, L0_attn_basis_k, L0_attn_basis_v, L0_attn_basis_o])
    phase = np.stack([L0_attn_phase_q, L0_attn_phase_k, L0_attn_phase_v, L0_attn_phase_o])
    amp = np.stack([L0_attn_amp_q, L0_attn_amp_k, L0_attn_amp_v, L0_attn_amp_o])
    given = {
        "x": L0_attn_hidden_states,
        "w_gate": w_gate, "w_up": w_up,
        "w_down": L0_ffn_w_down_proj.transpose(0, 2, 1).reshape(128, 6, 256),
        "w_router": L0_ffn_w_gate_router.reshape(8, 2, 128).transpose(2, 1, 0),
        "basis": basis.reshape(4, 64, 2, 128).transpose(3, 0, 2, 1),
        "phase": phase.reshape(2, 2, 256, 64).transpose(0, 3, 1, 2).reshape(128, 2, 256),
        "amp": amp.reshape(2, 2, 256, 64).transpose(0, 3, 1, 2).reshape(128, 2, 256),
    }
    nc = bacc.Bacc("TRN2", target_bir_lowering=False, num_devices=1,
                   dynamic_dma_scratch_size=1024)
    arrays, dram = {}, {}
    for name, a in given.items():
        arrays[f"{name}_in"] = np.ascontiguousarray(a)
        dram[name] = nc.dram_tensor(f"{name}_in", arrays[f"{name}_in"].shape, F32, kind="ExternalInput").ap()
    out = nc.dram_tensor("out", arrays["x_in"].shape, F32, kind="ExternalOutput").ap()
    macaron_block(nc, *(dram[name] for name in given), out)
    return run_bass_kernel_spmd(nc, [arrays], core_ids=[0]).results[0]["out"]
```
